# Optimizing a Trainium2 kernel written in Bass

```python
import numpy as np
import jax
import jax.numpy as jnp

def _softmax(x, axis=-1):
    return jax.nn.softmax(x, axis=axis)

def _gelu(x):
    return jax.nn.gelu(x, approximate=True)

def _silu(x):
    return jax.nn.silu(x)

def _sigmoid(x):
    return jax.nn.sigmoid(x)

def _layernorm(x, axis=-1, eps=1e-05):
    m = jnp.mean(x, axis=axis, keepdims=True)
    v = jnp.var(x, axis=axis, keepdims=True)
    return (x - m) / jnp.sqrt(v + eps)

def _scatter_add(tgt, idx, src, axis=0):
    return tgt.at[idx].add(src)

def _segment_sum(src, seg, n):
    return jax.ops.segment_sum(src, seg, n)
kernel_name = 'mk_sandwich_d1_jaxref_r8_52352d'

def setup_inputs(seed: int=0):
    np.random.seed(seed)
    _w = jnp.asarray

    def _L0_attn_setup():
        import jax, jax.numpy as jnp
        import numpy as np
        import math
        B, T, E = (2, 256, 256)
        G, QPG, D = (4, 4, 128)

        def sinusoidal_pe(t, d, dtype):
            pos = jnp.arange(t, dtype=jnp.float32)[:, None]
            i = jnp.arange(0, d, 2, dtype=jnp.float32)
            inv_freq = jnp.exp(-(jnp.log(10000.0) * i / d))
            ang = pos * inv_freq
            pe = jnp.zeros((t, d), dtype=jnp.float32)
            pe = pe.at[:, 0::2].set(jnp.sin(ang)).at[:, 1::2].set(jnp.cos(ang))
            return pe.astype(dtype)
        key = jax.random.key(seed)
        ks = jax.random.split(key, 6)
        s = lambda fan_in: 1.0 / math.sqrt(fan_in)
        return {'x': jax.random.normal(ks[0], (B, T, E), dtype=jnp.float32), 'wq': jax.random.uniform(ks[1], (E, G * QPG * D), jnp.float32, -s(E), s(E)), 'bq': jax.random.uniform(ks[2], (G * QPG * D,), jnp.float32, -s(E), s(E)), 'wkv': jax.random.uniform(ks[3], (E, 2 * G * D), jnp.float32, -s(E), s(E)), 'bkv': jax.random.uniform(ks[4], (2 * G * D,), jnp.float32, -s(E), s(E)), 'wo': jax.random.uniform(ks[5], (G * QPG * D, E), jnp.float32, -s(G * QPG * D), s(G * QPG * D))}
    _L0_attn_in = _L0_attn_setup()

    def _L0_ffn_setup():
        import jax, jax.numpy as jnp
        import numpy as np
        H = 256
        F = 176
        E = 64
        TOP_K = 6
        CAP = 64
        SCALE = 1.0
        F_SH = 2 * F
        B, S = (1, 256)
        key = jax.random.key(seed)
        ks = jax.random.split(key, 8)
        s = 0.02
        return {'hidden_states': jax.random.normal(ks[0], (B, S, H), jnp.float32), 'gate_w': jax.random.normal(ks[1], (E, H), jnp.float32) * s, 'w_gate': jax.random.normal(ks[2], (E, H, F), jnp.float32) * s, 'w_up': jax.random.normal(ks[3], (E, H, F), jnp.float32) * s, 'w_down': jax.random.normal(ks[4], (E, F, H), jnp.float32) * s, 'sh_gate': jax.random.normal(ks[5], (F_SH, H), jnp.float32) * s, 'sh_up': jax.random.normal(ks[6], (F_SH, H), jnp.float32) * s, 'sh_down': jax.random.normal(ks[7], (H, F_SH), jnp.float32) * s}
    _L0_ffn_in = _L0_ffn_setup()
    _d = {'L0_attn_x': _L0_attn_in['x'], 'L0_attn_wq': _L0_attn_in['wq'], 'L0_attn_bq': _L0_attn_in['bq'], 'L0_attn_wkv': _L0_attn_in['wkv'], 'L0_attn_bkv': _L0_attn_in['bkv'], 'L0_attn_wo': _L0_attn_in['wo'], 'L0_ffn_gate_w': _L0_ffn_in['gate_w'], 'L0_ffn_w_gate': _L0_ffn_in['w_gate'], 'L0_ffn_w_up': _L0_ffn_in['w_up'], 'L0_ffn_w_down': _L0_ffn_in['w_down'], 'L0_ffn_sh_gate': _L0_ffn_in['sh_gate'], 'L0_ffn_sh_up': _L0_ffn_in['sh_up'], 'L0_ffn_sh_down': _L0_ffn_in['sh_down']}
    _x0 = _d['L0_attn_x']
    _d['L0_attn_x'] = jax.random.normal(jax.random.fold_in(jax.random.key(seed), 1), (8, 512, 256), dtype=_x0.dtype)
    del _x0
    return _d

def reference(L0_attn_x, L0_attn_wq, L0_attn_bq, L0_attn_wkv, L0_attn_bkv, L0_attn_wo, L0_ffn_gate_w, L0_ffn_w_gate, L0_ffn_w_up, L0_ffn_w_down, L0_ffn_sh_gate, L0_ffn_sh_up, L0_ffn_sh_down):

    def _L0_attn_ref(x, wq, bq, wkv, bkv, wo):
        import jax, jax.numpy as jnp
        import numpy as np
        import math
        B, T, E = (2, 256, 256)
        G, QPG, D = (4, 4, 128)

        def sinusoidal_pe(t, d, dtype):
            pos = jnp.arange(t, dtype=jnp.float32)[:, None]
            i = jnp.arange(0, d, 2, dtype=jnp.float32)
            inv_freq = jnp.exp(-(jnp.log(10000.0) * i / d))
            ang = pos * inv_freq
            pe = jnp.zeros((t, d), dtype=jnp.float32)
            pe = pe.at[:, 0::2].set(jnp.sin(ang)).at[:, 1::2].set(jnp.cos(ang))
            return pe.astype(dtype)
        b, t, e = x.shape
        q = (x @ wq + bq).reshape(b, t, G, QPG, D).transpose(0, 2, 3, 1, 4)
        kv = (x @ wkv + bkv).reshape(b, t, G, 1, 2 * D).transpose(0, 2, 3, 1, 4)
        k, v = (kv[..., :D], kv[..., D:])
        pe = sinusoidal_pe(t, D, x.dtype)
        q = q + pe
        k = k + pe
        scores = jnp.einsum('bgqtd,bgksd->bgqts', q, k) / math.sqrt(D)
        causal = jnp.tril(jnp.ones((t, t), dtype=bool))
        scores = jnp.where(causal, scores, -jnp.inf)
        probs = jax.nn.softmax(scores, axis=-1)
        out = jnp.einsum('bgqts,bgksd->btgqd', probs, v).reshape(b, t, G * QPG * D)
        return out @ wo

    def _L0_ffn_ref(hidden_states, gate_w, w_gate, w_up, w_down, sh_gate, sh_up, sh_down):
        import jax, jax.numpy as jnp
        import numpy as np
        H = 256
        F = 176
        E = 64
        TOP_K = 6
        CAP = 64
        SCALE = 1.0
        F_SH = 2 * F
        B, S = (1, 256)
        b, s, _ = hidden_states.shape
        x = hidden_states.reshape(-1, H)
        T = x.shape[0]
        logits = x.astype(jnp.float32) @ gate_w.astype(jnp.float32).T
        scores = jax.nn.softmax(logits, axis=-1)
        topk_w, topk_idx = jax.lax.top_k(scores, TOP_K)
        topk_w = topk_w * SCALE
        eid = topk_idx.reshape(-1)
        x_exp = jnp.repeat(x, TOP_K, axis=0)
        order = jnp.argsort(eid)
        eid_s = eid[order]
        counts = jnp.bincount(eid, length=E)
        starts = jnp.cumsum(counts) - counts
        pos = jnp.arange(T * TOP_K) - starts[eid_s]
        valid = pos < CAP
        pos_c = jnp.where(valid, pos, CAP)
        buf = jnp.zeros((E, CAP + 1, H), x.dtype).at[eid_s, pos_c].set(x_exp[order])
        g = jax.nn.silu(jnp.einsum('ech,ehf->ecf', buf, w_gate))
        u = jnp.einsum('ech,ehf->ecf', buf, w_up)
        d = jnp.einsum('ecf,efh->ech', g * u, w_down)
        out_s = jnp.where(valid[:, None], d[eid_s, pos_c], 0.0)
        out_exp = jnp.zeros_like(out_s).at[order].set(out_s)
        y = jnp.einsum('tkh,tk->th', out_exp.reshape(T, TOP_K, H), topk_w)
        y = y.astype(x.dtype).reshape(b, s, H)
        gs = jax.nn.silu(hidden_states @ sh_gate.T)
        us = hidden_states @ sh_up.T
        y = y + gs * us @ sh_down.T
        return y
    x = L0_attn_x
    x = x + _layernorm(_L0_attn_ref(_layernorm(x, axis=-1), L0_attn_wq, L0_attn_bq, L0_attn_wkv, L0_attn_bkv, L0_attn_wo), axis=-1)
    x = x + _layernorm(_L0_ffn_ref(_layernorm(x, axis=-1), L0_ffn_gate_w, L0_ffn_w_gate, L0_ffn_w_up, L0_ffn_w_down, L0_ffn_sh_gate, L0_ffn_sh_up, L0_ffn_sh_down), axis=-1)
    return x

_drawn_inputs = setup_inputs


def setup_inputs(seed=0):
    import zlib

    import numpy as np

    out = dict(_drawn_inputs(seed))
    spreads = {}
    factors = {'L0_attn_bq': 2.822,
     'L0_ffn_gate_w': 3.506,
     'L0_ffn_w_gate': 2.861,
     'L0_ffn_w_up': 2.748,
     'L0_ffn_w_down': 2.758}
    for name, (base, spread) in spreads.items():
        noise = np.random.default_rng([zlib.crc32(name.encode()), seed]).standard_normal(out[name].shape)
        drawn = base * np.exp(spread * noise) if base else spread * noise
        out[name] = jnp.asarray(drawn.astype(out[name].dtype))
    for name, factor in factors.items():
        out[name] = (out[name] * factor).astype(out[name].dtype)
    return out
```

```python
from contextlib import ExitStack

import concourse.bass as bass
from concourse import mybir

F32 = mybir.dt.float32
F32R = mybir.dt.float32r
BF16 = mybir.dt.bfloat16
I32 = mybir.dt.int32
U32 = mybir.dt.uint32
ALU = mybir.AluOpType
ACT = mybir.ActivationFunctionType
AX = mybir.AxisListType.X

P = 128
TOP_K = 6
CAP = 64
EPS = 1e-5
MAGIC = 0x5F3759DF
BIG = 3.0e38
MASKED = -1.0e30


class Queue:

    def __init__(self, sem):
        self.sem, self.count, self.steps, self.seen = sem, 0, [], {}

    def wait(self, *tokens):
        for token in tokens:
            if token is None:
                continue
            if isinstance(token, list):
                self.wait(*token)
                continue
            sem, value = token
            if self.seen.get(sem.name, 0) < value:
                self.seen[sem.name] = value
                self.steps.append(lambda e, s=sem, v=value: e.wait_ge(s, v))

    def run(self, make):
        self.steps.append(make)

    def done(self, make):
        self.count += 1
        self.steps.append(lambda e, s=self.sem: make(e).then_inc(s, 1))
        return self.sem, self.count

    def emit(self, engine):
        for step in self.steps:
            step(engine)


class Slot:

    def __init__(self, sem):
        self.sem, self.count = sem, 0

    def start(self, queue, out, in_):
        self.count += 16
        queue.steps.append(lambda e, s=self.sem: e.dma_start(out, in_).then_inc(s, 16))
        return self.sem, self.count


def build(nc, x, wq, bqT, wkv, bkvT, wo, gwT, w_gate, w_up, w_down, sgT, suT, sdT, consts, out):
    NB, T, E = x.shape
    NQ = wq.shape[1] // P
    NG = wkv.shape[1] // (2 * P)
    QPG = NQ // NG
    TT = T // P
    EC = E // P
    NE, _, F = w_gate.shape
    FS = sgT.shape[1]
    NT = NB * T
    FCH = [(f, min(P, FS - f)) for f in range(0, FS, P)]
    HT = T // 2
    F2 = F // 2
    ROW = E + NE
    TRASH = CAP
    SUMROWS = NT + TRASH
    S4 = float(P) ** -0.25
    assert T == 512 and E == 256 and F % 2 == 0 and NE == 64

    table = nc.dram_tensor("token_table", [NT + 1, ROW], F32, kind="Internal").ap()
    x2_dram = nc.dram_tensor("x2_rows", [NT, E], F32, kind="Internal").ap()
    sums = nc.dram_tensor("ffn_sums", [2 * SUMROWS, E], F32, kind="Internal").ap()

    with ExitStack() as ctx:
        def sem(name):
            return ctx.enter_context(nc.semaphore(name))

        at = [0]
        base = nc.sbuf_usable_end - nc.sbuf_bytes_remaining
        at[0] = (base + 31) // 32 * 32

        def place(name, shape, dt):
            size = 4 if dt in (F32, F32R, I32, U32) else 2
            for n in shape[1:]:
                size *= n
            t = nc.alloc_sbuf_tensor_at(name, shape, dt, offset=at[0])
            at[0] += (size + 31) // 32 * 32
            return t

        weights_at = at[0]
        wq_h, wq_l = (place(f"wq_{s}", [P, EC, NQ * P], F32R) for s in "hl")
        wkv_h, wkv_l = (place(f"wkv_{s}", [P, EC, 2 * NG * P], F32R) for s in "hl")
        wkv_end = at[0]
        wo_h, wo_l = (place(f"wo_{s}", [P, NQ, E], F32R) for s in "hl")
        weights_end = at[0]
        sg_h, sg_l = (place(f"sg_{s}", [P, EC, FS], F32R) for s in "hl")
        su_h, su_l = (place(f"su_{s}", [P, EC, FS], F32R) for s in "hl")
        sd_h, sd_l = (place(f"sd_{s}", [P, len(FCH), E], F32R) for s in "hl")
        gw_h, gw_l = (place(f"gw_{s}", [P, EC, NE], F32R) for s in "hl")
        ident = place("ident", [P, P], F32)
        pe_t = place("pe_t", [P, T], F32)
        key_row = place("key_row", [P, HT], F32)
        slot_row = place("slot_row", [P, CAP], F32)
        ident_b = place("ident_b", [P, P], BF16)
        causal_b = place("causal_b", [P, P], BF16)
        bq_s = place("bq_s", [P, NQ], F32)
        bkv_s = place("bkv_s", [P, 2 * NG], F32)
        bk4 = place("bk4", [P, 2 * NG], F32)
        work_at = at[0]
        xn_h, xn_l = (place(f"xn_{s}", [P, EC, T], F32R) for s in "hl")
        k_h, k_l = (place(f"k_{s}", [P, NG, T], F32R) for s in "hl")
        v_h, v_l = (place(f"v_{s}", [P, TT, NG * P], F32R) for s in "hl")
        stage_at = at[0]
        q_sum = place("q_sum", [P, T], F32)
        q_h, q_l = (place(f"q_{s}", [P, 2, T], F32R) for s in "hl")
        tri = [P * (i * (i + 1) // 2) for i in range(TT + 1)]
        inv = [P * (TT * j - j * (j - 1) // 2) for j in range(TT + 1)]
        prob = place("prob", [P, 2, tri[TT]], F32)
        pt_h, pt_l = (place(f"pt_{s}", [P, tri[TT]], F32R) for s in "hl")
        o_h, o_l = (place(f"o_{s}", [P, T], F32R) for s in "hl")
        negmax = place("negmax", [P, 2, TT], F32)
        rsum = place("rsum", [P, 2, TT], F32)
        rinv = place("rinv", [P, 2, TT], F32)
        stage_end = at[0]
        xio = place("xio", [P, TT, E], F32)
        ytr = place("ytr", [P, EC, T], F32)
        rows = place("rows", [P, TT, ROW], F32)
        x2_h, x2_l = (place(f"x2_{s}", [P, EC, HT], F32R) for s in "hl")
        logit = place("logit", [P, 2, NE + 2], F32)
        top8 = place("top8", [P, 2, 8], F32)
        left = place("left", [P, 2, NE + 2], F32)
        mask = place("mask", [P, 2, NE], F32)
        rmax = place("rmax", [P, 2], F32)
        psum_ = place("router_sum", [P, 2], F32)
        pinv = place("router_inv", [P, 2], F32)
        sig = place("sig", [P, HT], F32)
        act = place("act", [P, HT], F32)
        a_h, a_l = (place(f"a_{s}", [P, len(FCH), HT], F32R) for s in "hl")
        keys = place("keys", [P, CAP + T], F32)
        first = place("first", [P, CAP], F32)
        stat = place("stat", [P, TT, 6], F32)
        mv = place("mv", [P, TT, 2], F32)
        nw = place("nw", [P, 4, TT], F32)
        end_at = at[0]
        assert end_at <= nc.sbuf_usable_end, (end_at, nc.sbuf_usable_end)
        at[0] = stage_at
        STG = 2048
        stage = [place(f"stage{i}", [P, STG], F32) for i in range(3)]
        causal_f = place("causal_f", [P, P], F32)
        zero_f = place("zero_f", [P, 2048], F32)
        assert at[0] <= stage_end
        at[0] = weights_at
        NW = 16
        w_gu, w_dn = [], []
        w_where = []
        for s in range(NW):
            w_gu.append(place(f"w_gu{s}", [P, 2, 2 * F], F32))
            w_dn.append(place(f"w_dn{s}", [P, 2, E], F32))
            w_where.append(at[0])
        assert at[0] <= weights_end
        at[0] = work_at
        NX = 4
        xg = [place(f"xg{i}", [P, ROW], F32) for i in range(NX)]
        xt = [place(f"xt{i}", [P, EC, P], F32) for i in range(2)]
        ex = [place(f"ex{i}", [P, F], F32) for i in range(2)]
        ag = [place(f"ag{i}", [P, F], F32) for i in range(2)]
        atr = [place(f"atr{i}", [P, 2, P], F32) for i in range(2)]
        dsum = [place(f"dsum{i}", [P, E], F32) for i in range(2)]
        tok2 = place("tok2", [P, 2 * CAP], F32)
        sct2 = place("sct2", [P, 2 * CAP], F32)
        empty = place("empty", [P, CAP], F32)
        idx_g = place("idx_g", [P, NE // 2], I32)
        idx_s = place("idx_s", [P, NE // 2], I32)
        NF = 3
        fa = [place(f"fa{i}", [P, TT, E], F32) for i in range(NF)]
        fb = [place(f"fb{i}", [P, TT, E], F32) for i in range(NF)]
        fx = [place(f"fx{i}", [P, TT, E], F32) for i in range(NF)]
        fstat = place("fstat", [P, TT, 6], F32)
        fmv = place("fmv", [P, TT, 2], F32)
        fnw = place("fnw", [P, 4, TT], F32)
        assert at[0] <= end_at - 4 * (CAP + T + CAP + 64)

        bank = {n: ctx.enter_context(nc.psum_tensor(f"bank_{n}", [P, 512], F32))
                for n in ("s0", "s1", "t0", "t1", "o", "y0", "y1", "f")}
        free = {n: None for n in bank}

        pe, dve, actq, pool, sp = (Queue(sem(f"{n}_done")) for n in ("pe", "dve", "act", "pool", "sp"))

        def mm(o, l, r, start=False, stop=False, last=False):
            def make(e):
                return e.matmul(o, l, r, start=start, stop=stop, skip_group_check=True)
            return pe.done(make) if last else pe.run(make)

        def mm3(o, l, r, start, last=False):
            mm(o, l[0], r[0], start=start)
            mm(o, l[0], r[1])
            return mm(o, l[1], r[0], stop=True, last=last)

        def tr(o, i, idn, last=False):
            def make(e):
                return e.transpose(o, i, idn)
            return pe.done(make) if last else pe.run(make)

        def f(ap):
            return ap.bitcast(F32)

        s_const, s_zero = Slot(sem("dma_const")), Slot(sem("dma_zero"))
        s_stage = [Slot(sem(f"dma_stage{i}")) for i in range(3)]
        s_x = Slot(sem("dma_x"))
        x_rows = x.rearrange("b (i p) e -> b p i e", p=P)

        def load_x(b, *before):
            sp.wait(*before)
            return s_x.start(sp, xio[:], x_rows[b])

        x_in = load_x(0)
        C = consts
        c0 = 0
        for t, n in ((ident, P), (pe_t, T), (key_row, HT), (slot_row, CAP), (causal_f, P)):
            const_in = s_const.start(sp, t[:, 0:n], C[:, c0:c0 + n])
            c0 += n
        s_const.start(sp, bq_s[:], bqT)
        const_in = s_const.start(sp, bkv_s[:], bkvT)

        def dup(pair, shape_view):
            return [shape_view(t) for t in pair]

        pieces = []
        kv = wkv.rearrange("(c p) (g two d) -> p c g two d", p=P, two=2, d=P)
        for c in range(EC):
            pieces.append(([(wkv[c * P:(c + 1) * P, :], 0, 2 * NG * P)], P, [
                (0, 2 * NG * P, [t[:, c, :] for t in (wkv_h, wkv_l)], "kv")]))
        for c in range(EC):
            pieces.append(([(wq[c * P:(c + 1) * P, :], 0, NQ * P)], P, [
                (0, NQ * P, [t[:, c, :] for t in (wq_h, wq_l)], S4)]))
        for c in range(2):
            n = NQ // 2
            pieces.append(([(wo[c * n * P:(c + 1) * n * P, :].rearrange("(h p) e -> p h e", p=P), 0, n * E)], P, [
                (0, n * E, [t[:, c * n:(c + 1) * n, :].rearrange("p h e -> p (h e)") for t in (wo_h, wo_l)], 1.0)]))
        pieces.append(([(sgT.rearrange("(c p) f -> p c f", p=P), 0, EC * FS),
                        (suT.rearrange("(c p) f -> p c f", p=P), EC * FS, EC * FS),
                        (gwT.rearrange("(c p) f -> p c f", p=P), 2 * EC * FS, EC * NE)], P, [
            (0, EC * FS, [t[:, :, :].rearrange("p c f -> p (c f)") for t in (sg_h, sg_l)], 1.0),
            (EC * FS, EC * FS, [t[:, :, :].rearrange("p c f -> p (c f)") for t in (su_h, su_l)], 1.0),
            (2 * EC * FS, EC * NE, [t[:, :, :].rearrange("p c f -> p (c f)") for t in (gw_h, gw_l)], 1.0)]))
        whole = [q for q in FCH if q[1] == P]
        pieces.append(([(sdT[0:P * len(whole), :].rearrange("(c p) e -> p c e", p=P), 0, len(whole) * E)], P, [
            (0, len(whole) * E, [t[:, 0:len(whole), :].rearrange("p c e -> p (c e)") for t in (sd_h, sd_l)], 1.0)]))
        if len(whole) < len(FCH):
            r0, rn = FCH[-1]
            pieces.append(([(sdT[r0:r0 + rn, :], 0, E)], rn, [
                (0, E, [t[0:rn, len(whole), :] for t in (sd_h, sd_l)], 1.0)]))

        stage_free = [None] * 3
        split = []

        def load_piece(n):
            sources, rowsn, _ = pieces[n]
            sp.wait(stage_free[n % 3])
            for src, a, w in sources:
                dst = stage[n % 3][0:rowsn, a:a + w]
                if len(src.shape) == 3:
                    dst = dst.rearrange("p (c f) -> p c f", c=src.shape[1])
                tok = s_stage[n % 3].start(sp, dst, src)
            return tok

        def split_piece(n, tok):
            _, rowsn, parts = pieces[n]
            actq.wait(tok)
            dve.wait(tok)
            for a, w, (hi, lo), scale in parts:
                src = stage[n % 3][0:rowsn, a:a + w]
                todo = [(src, hi, lo, scale)]
                if scale == "kv":
                    v = [t.rearrange("p (g two d) -> p g two d", two=2, d=P) for t in (src, hi, lo)]
                    todo = [(*[t[:, :, k, :] for t in v], (S4, 1.0)[k]) for k in range(2)]
                for s_, h_, l_, m_ in todo:
                    t1 = actq.done(lambda e, s_=s_, h_=h_, m_=m_: e.activation(h_, s_, ACT.Copy, scale=m_))
                    dve.wait(t1)
                    t2 = dve.done(lambda e, s_=s_, h_=h_, l_=l_, m_=m_: e.scalar_tensor_tensor(
                        out=l_, in0=s_, scalar=m_, in1=f(h_), op0=ALU.mult, op1=ALU.subtract))
            stage_free[n % 3] = t2
            split.append(t2)

        toks = [load_piece(n) for n in range(3)]
        dve.wait(const_in)
        dve.run(lambda e: e.tensor_copy(ident_b[:], ident[:]))
        dve.run(lambda e: e.tensor_copy(causal_b[:], causal_f[:]))
        dve.run(lambda e: e.memset(logit[:, :, NE:NE + 2], BIG))
        dve.run(lambda e: e.memset(keys[0:NE, 0:CAP], 0.0))
        zeroed = dve.done(lambda e: e.memset(zero_f[:], 0.0))
        dve.run(lambda e: e.tensor_scalar(bk4[:], bkv_s[:], S4, None, ALU.mult))
        dve.wait(zeroed)
        bq_ready = dve.done(lambda e: e.tensor_scalar(bq_s[:], bq_s[:], S4, None, ALU.mult))
        dve.wait(bq_ready)

        def newton(mvt, nwt, n0, n):
            v, y, a = nwt[:, 0, n0:n0 + n], nwt[:, 1, n0:n0 + n], nwt[:, 2, n0:n0 + n]
            var = mvt[:, n0:n0 + n, 1:2].rearrange("p i o -> p (i o)")

            def step(make):
                dve.wait(dve.done(make))
            step(lambda e: e.tensor_scalar(v, var, EPS, None, ALU.add))
            step(lambda e: e.tensor_scalar(a.bitcast(I32), v.bitcast(I32), 1, None, ALU.logical_shift_right))
            step(lambda e: e.tensor_scalar(y.bitcast(I32), a.bitcast(I32), -1.0, float(MAGIC), ALU.mult, ALU.add))
            for _ in range(3):
                step(lambda e: e.tensor_tensor(a, y, y, ALU.mult))
                step(lambda e: e.scalar_tensor_tensor(out=a, in0=a, scalar=-0.5, in1=v, op0=ALU.mult, op1=ALU.mult))
                step(lambda e: e.scalar_tensor_tensor(out=y, in0=a, scalar=1.5, in1=y, op0=ALU.add, op1=ALU.mult))

        def statistics(sources, statt, mvt, nwt, n0):
            n = len(sources)
            for i, s_ in enumerate(sources):
                t = dve.done(lambda e, s_=s_, i=i: e.bn_stats(statt[:, n0 + i, :], s_))
            dve.wait(t)
            for i in range(n):
                t = dve.done(lambda e, i=i: e.bn_aggr(mvt[:, n0 + i, :], statt[:, n0 + i, :]))
            dve.wait(t)
            newton(mvt, nwt, n0, n)

        def normed(o, s_, mvt, nwt, i):
            return dve.done(lambda e: e.tensor_scalar(o, s_, mvt[:, i, 0:1], nwt[:, 1, i:i + 1],
                                                      ALU.subtract, ALU.mult))

        ready = {}
        last_read = {}

        def norm_x():
            dve.wait(x_in)
            statistics([xio[:, i, :] for i in range(TT)], stat, mv, nw, 0)
            for i in range(TT):
                t = normed(xio[:, i, :], xio[:, i, :], mv, nw, i)
            ready["xnorm"] = t

        def turn_x(c, bk):
            pe.wait(ready["xnorm"], free[bk], const_in)
            for i in range(TT):
                t = tr(bank[bk][:, i * P:(i + 1) * P], xio[:, i, c * P:(c + 1) * P], ident[:], last=i == TT - 1)
            last_read["xio"] = t
            actq.wait(t, last_read.get("xn"))
            t = actq.done(lambda e: e.activation(xn_h[:, c, :], bank[bk][:], ACT.Copy))
            dve.wait(t)
            t = dve.done(lambda e: e.tensor_tensor(xn_l[:, c, :], bank[bk][:], f(xn_h[:, c, :]), ALU.subtract))
            free[bk] = ready["xn"] = t

        def project(bk, hi, lo, col):
            pe.wait(free[bk], ready["xn"])
            for c in range(EC):
                t = mm3(bank[bk][:], [w[:, c, col:col + P] for w in (hi, lo)],
                        [a[:, c, :] for a in (xn_h, xn_l)], start=c == 0, last=c == EC - 1)
            last_read["xn"] = t
            return t

        def with_position(bk, t, bias, h_, l_, before):
            dve.wait(t, last_read.get("q_sum"))
            t = dve.done(lambda e: e.scalar_tensor_tensor(out=q_sum[:], in0=bank[bk][:], scalar=bias,
                                                          in1=pe_t[:], op0=ALU.add, op1=ALU.add))
            free[bk] = t
            actq.wait(t, before)
            t = actq.done(lambda e: e.activation(h_, q_sum[:], ACT.Copy))
            pool.wait(t)
            t = pool.done(lambda e: e.tensor_tensor(l_, q_sum[:], f(h_), ALU.subtract))
            last_read["q_sum"] = t
            return t

        def make_k(g, bk):
            pe.wait(split[1])
            t = project(bk, wkv_h, wkv_l, 2 * g * P)
            ready["k", g] = with_position(bk, t, bk4[:, 2 * g:2 * g + 1], k_h[:, g, :], k_l[:, g, :],
                                          last_read.get(("k", g)))

        def make_v(half, s2, bk):
            pe.wait(free[bk], ready["xn"], split[1])
            ng = NG // 2
            g0 = half * ng
            views = [w[:, :, :].rearrange("p c (g two d) -> p c g two d", two=2, d=P)[:, :, g0:g0 + ng, 1, :]
                     for w in (wkv_h, wkv_l)]
            for k in range(2):
                s = 2 * s2 + k
                o = bank[bk][:, k * ng * P:(k + 1) * ng * P]
                for c in range(EC):
                    t = mm3(o, [a[:, c, s * P:(s + 1) * P] for a in (xn_h, xn_l)],
                            [w[:, c] for w in views], start=c == 0, last=c == EC - 1)
            last_read["xn"] = t
            src = bank[bk][:].rearrange("p (s n) -> p s n", s=2)
            h_, l_ = (v[:, 2 * s2:2 * s2 + 2, g0 * P:(g0 + ng) * P] for v in (v_h, v_l))
            actq.wait(t, last_read.get(("v", half)))
            t = actq.done(lambda e: e.activation(h_, src, ACT.Copy))
            dve.wait(t)
            t = dve.done(lambda e: e.tensor_tensor(l_, src, f(h_), ALU.subtract))
            free[bk] = ready["v", half] = t

        def make_q(n):
            h = n % NQ
            pe.wait(split[3])
            t = project("f", wq_h, wq_l, h * P)
            ready["q", n] = with_position("f", t, bq_s[:, h:h + 1], q_h[:, n % 2, :], q_l[:, n % 2, :],
                                          last_read.get(("q", n - 2)))

        def scores(n, i):
            h, r = n % NQ, n % 2
            g, w, bk = h // QPG, (i + 1) * P, f"s{i % 2}"
            pe.wait(free[bk], ready["q", n], ready["k", g])
            mm(bank[bk][:, i * P:w], ident_b[:], causal_b[:], start=True)
            t = mm3(bank[bk][:, 0:w], [q[:, r, i * P:(i + 1) * P] for q in (q_h, q_l)],
                    [k[:, g, 0:w] for k in (k_h, k_l)], start=False, last=True)
            last_read["q", n] = last_read["k", g] = t
            dve.wait(t, ready.get(("exp", n - 2, i)))
            t = dve.done(lambda e: e.reduce_max(negmax[:, r, i:i + 1], bank[bk][:, 0:w], AX, negate=True))
            actq.wait(t, ready.get(("turned", n - 2)), ready.get(("rinv", n - 2, i)))
            t = actq.done(lambda e: e.activation(prob[:, r, tri[i]:tri[i + 1]], bank[bk][:, 0:w], ACT.Exp,
                                                 bias=negmax[:, r, i:i + 1], accum_out=rsum[:, r, i:i + 1]))
            free[bk] = ready["exp", n, i] = t

        def normalise(n, i):
            r = n % 2
            dve.wait(ready["exp", n, i], ready.get(("normal", n - 2, i)))
            t = dve.done(lambda e: e.reciprocal(rinv[:, r, i:i + 1], rsum[:, r, i:i + 1]))
            ready["rinv", n, i] = t
            pool.wait(t)
            p_ = prob[:, r, tri[i]:tri[i + 1]]
            w = (i + 1) * P
            ready["normal", n, i] = pool.done(lambda e: e.tensor_tensor(
                p_, p_, rinv[:, r, i:i + 1].to_broadcast([P, w]), ALU.mult))

        def turn(n, j):
            r, bk, w = n % 2, f"t{j % 2}", (TT - j) * P
            pe.wait(free[bk], [ready["normal", n, i] for i in range(j, TT)])
            for i in range(j, TT):
                t = tr(bank[bk][:, (i - j) * P:(i - j + 1) * P],
                       prob[:, r, tri[i] + j * P:tri[i] + (j + 1) * P], ident[:], last=i == TT - 1)
            if j == 0:
                ready["turned", n] = t
            h_, l_ = (q[:, inv[j]:inv[j + 1]] for q in (pt_h, pt_l))
            actq.wait(t, last_read.get(("pt", j)))
            t = actq.done(lambda e: e.activation(h_, bank[bk][:, 0:w], ACT.Copy))
            dve.wait(t)
            t = dve.done(lambda e: e.tensor_tensor(l_, bank[bk][:, 0:w], f(h_), ALU.subtract))
            free[bk] = ready["pt", n, j] = t

        def values(n, j):
            h = n % NQ
            g = h // QPG
            pe.wait(ready["pt", n, j], ready["v", g // (NG // 2)])
            if j == TT - 1:
                pe.wait(free["o"])
            t = mm3(bank["o"][:, j * P:T], [v[:, j, g * P:(g + 1) * P] for v in (v_h, v_l)],
                    [q[:, inv[j]:inv[j + 1]] for q in (pt_h, pt_l)], start=j == TT - 1, last=True)
            last_read["pt", j] = last_read["v", g // (NG // 2)] = t
            if j == 0:
                bias = bkv_s[:, 2 * g + 1:2 * g + 2]
                actq.wait(t, last_read.get("o"))
                t = actq.done(lambda e: e.activation(o_h[:], bank["o"][:], ACT.Identity, bias=bias))
                dve.wait(t)
                t = dve.done(lambda e: e.scalar_tensor_tensor(out=o_l[:], in0=bank["o"][:], scalar=bias,
                                                              in1=f(o_h[:]), op0=ALU.add, op1=ALU.subtract))
                free["o"] = ready["o", n] = t

        def project_out(n):
            h = n % NQ
            pe.wait(ready["o", n], split[5])
            if h == 0:
                pe.wait(free["y0"], free["y1"])
            for c in range(EC):
                t = mm3(bank[f"y{c}"][:], [w[:, h, c * P:(c + 1) * P] for w in (wo_h, wo_l)],
                        [o_h[:], o_l[:]], start=h == 0, last=c == EC - 1)
            last_read["o"] = t
            if h == NQ - 1:
                actq.wait(t, last_read.get("ytr"))
                dve.wait(t, last_read.get("ytr"))
                free["y0"] = actq.done(lambda e: e.activation(ytr[:, 0, :], bank["y0"][:], ACT.Copy))
                free["y1"] = dve.done(lambda e: e.tensor_copy(ytr[:, 1, :], bank["y1"][:]))
                ready["ytr"] = [free["y0"], free["y1"]]

        s_x2, s_rows, s_ffn = Slot(sem("dma_x2")), Slot(sem("dma_rows")), [Slot(sem(f"dma_ffn{k}")) for k in range(2)]
        stored = {}
        x2_rows = x2_dram.rearrange("(b i p) e -> b p i e", p=P, i=TT)
        table_rows = table[0:NT, :].rearrange("(b i p) e -> b p i e", p=P, i=TT)
        sum_rows = [sums[a * SUMROWS:a * SUMROWS + NT, :].rearrange("(b i p) e -> b p i e", p=P, i=TT)
                    for a in range(2)]

        def token_layer(b):
            x_again = load_x(b, last_read["xio"])
            for k in range(2):
                pe.wait(free["f"], ready["ytr"])
                for i in range(2):
                    for c in range(EC):
                        t = tr(bank["f"][:, i * E + c * P:i * E + (c + 1) * P],
                               ytr[:, c, (2 * k + i) * P:(2 * k + i + 1) * P], ident[:],
                               last=(i, c) == (1, EC - 1))
                last_read["ytr"] = t
                dve.wait(t, stored.get("rows"))
                src = [bank["f"][:, i * E:(i + 1) * E] for i in range(2)]
                statistics(src, stat, mv, nw, 2 * k)
                for i in range(2):
                    t = normed(rows[:, 2 * k + i, 0:E], src[i], mv, nw, 2 * k + i)
                free["f"] = t
                pool.wait(t, x_again)
                for i in range(2):
                    s_, o_ = rows[:, 2 * k + i, 0:E], xio[:, 2 * k + i, :]
                    t = pool.done(lambda e, s_=s_, o_=o_: e.tensor_tensor(o_, o_, s_, ALU.add))
                yield
                dve.wait(t)
                statistics([xio[:, 2 * k + i, :] for i in range(2)], stat, mv, nw, 2 * k)
                for i in range(2):
                    t = normed(rows[:, 2 * k + i, 0:E], xio[:, 2 * k + i, :], mv, nw, 2 * k + i)
                ready["ln2", k] = t
            sp.wait(t)
            stored["x2"] = s_x2.start(sp, x2_rows[b], xio[:])
            last_read["xio"] = stored["x2"]
            for k in range(2):
                pe.wait(ready["ln2", k], free["f"])
                for c in range(EC):
                    for i in range(2):
                        t = tr(bank["f"][:, c * HT + i * P:c * HT + (i + 1) * P],
                               rows[:, 2 * k + i, c * P:(c + 1) * P], ident[:], last=(c, i) == (EC - 1, 1))
                src = bank["f"][:].rearrange("p (c t) -> p c t", c=EC)
                actq.wait(t, last_read.get("x2"))
                t = actq.done(lambda e, src=src: e.activation(x2_h[:], src, ACT.Copy))
                dve.wait(t)
                t = dve.done(lambda e, src=src: e.tensor_tensor(x2_l[:], src, f(x2_h[:]), ALU.subtract))
                free["f"] = ready["x2"] = t
                yield
                pe.wait(ready["x2"], free["f"], split[6])
                for i in range(2):
                    for c in range(EC):
                        t = mm3(bank["f"][:, i * NE:(i + 1) * NE],
                                [a[:, c, i * P:(i + 1) * P] for a in (x2_h, x2_l)],
                                [w[:, c, :] for w in (gw_h, gw_l)], start=c == 0, last=c == EC - 1)
                dve.wait(t)
                t = dve.done(lambda e: e.tensor_copy(logit[:, :, 0:NE], bank["f"][:, 0:2 * NE].rearrange(
                    "p (i n) -> p i n", i=2)))
                free["f"] = t
                dve.wait(t)
                for i in range(2):
                    t = dve.done(lambda e, i=i: e.max(top8[:, i, :], logit[:, i, :]))
                dve.wait(t)
                for i in range(2):
                    t = dve.done(lambda e, i=i: e.match_replace(left[:, i, :], top8[:, i, :], logit[:, i, :], -BIG))
                dve.wait(ready.get("router_exp"))
                t2 = dve.done(lambda e: e.tensor_scalar(rmax[:], top8[:, :, 2:3].rearrange("p i o -> p (i o)"),
                                                        -1.0, None, ALU.mult))
                dve.wait(t, last_read.get("mask"))
                ready["mask"] = dve.done(lambda e: e.tensor_scalar(mask[:], left[:, :, 0:NE], -BIG, None,
                                                                   ALU.is_equal))
                actq.wait(t2)
                for i in range(2):
                    o_ = rows[:, 2 * k + i, E:ROW]
                    t = actq.done(lambda e, i=i, o_=o_: e.activation(o_, logit[:, i, 0:NE], ACT.Exp,
                                                                     bias=rmax[:, i:i + 1],
                                                                     accum_out=psum_[:, i:i + 1]))
                ready["router_exp"] = t
                yield
                dve.wait(ready["router_exp"])
                t = dve.done(lambda e: e.reciprocal(pinv[:], psum_[:]))
                dve.wait(t)
                for i in range(2):
                    o_ = rows[:, 2 * k + i, E:ROW]
                    t = dve.done(lambda e, i=i, o_=o_: e.tensor_scalar(o_, o_, pinv[:, i:i + 1], None, ALU.mult))
                if k == 1:
                    sp.wait(t)
                    stored["rows"] = s_rows.start(sp, table_rows[b], rows[:])
                pe.wait(ready["mask"], free["f"])
                for i in range(2):
                    t = tr(bank["f"][0:NE, i * P:(i + 1) * P], mask[:, i, :], ident[:], last=i == 1)
                last_read["mask"] = t
                off = float(NT - b * T - k * HT)
                o_ = keys[0:NE, CAP + k * HT:CAP + (k + 1) * HT]
                dve.wait(t)
                t = dve.done(lambda e, off=off, o_=o_: e.scalar_tensor_tensor(
                    out=o_, in0=key_row[0:NE, :], scalar=off, in1=bank["f"][0:NE, 0:HT],
                    op0=ALU.add, op1=ALU.mult))
                free["f"] = ready["keys"] = t
                yield
                for n, (f0, fn) in enumerate(FCH):
                    pe.wait(free["f"], ready["x2"], split[-1])
                    for u, (hi, lo) in enumerate(((sg_h, sg_l), (su_h, su_l))):
                        for c in range(EC):
                            t = mm3(bank["f"][0:fn, u * HT:(u + 1) * HT], [w[:, c, f0:f0 + fn] for w in (hi, lo)],
                                    [a[:, c, :] for a in (x2_h, x2_l)], start=c == 0, last=c == EC - 1)
                    last_read["x2"] = t
                    gate, up = bank["f"][0:fn, 0:HT], bank["f"][0:fn, HT:2 * HT]
                    s_, a_ = sig[0:fn, :], act[0:fn, :]
                    actq.wait(t, ready.get("act"))
                    t = actq.done(lambda e, s_=s_, gate=gate: e.activation(s_, gate, ACT.Exp, scale=-1.0))
                    dve.wait(t)
                    t = dve.done(lambda e, s_=s_: e.tensor_scalar(s_, s_, 1.0, None, ALU.add))
                    dve.wait(t)
                    t = dve.done(lambda e, s_=s_: e.reciprocal(s_, s_))
                    dve.wait(t)
                    t = dve.done(lambda e, s_=s_, gate=gate: e.tensor_tensor(s_, gate, s_, ALU.mult))
                    dve.wait(t, last_read.get("act"))
                    t = dve.done(lambda e, s_=s_, a_=a_, up=up: e.tensor_tensor(a_, up, s_, ALU.mult))
                    free["f"] = ready["act"] = t
                    h_, l_ = (q[0:fn, n, :] for q in (a_h, a_l))
                    actq.wait(t, last_read.get("a"))
                    t = actq.done(lambda e, h_=h_, a_=a_: e.activation(h_, a_, ACT.Copy))
                    pool.wait(t)
                    t = pool.done(lambda e, l_=l_, h_=h_, a_=a_: e.tensor_tensor(l_, a_, f(h_), ALU.subtract))
                    last_read["act"] = t
                    ready["a"] = t
                    yield
                pe.wait(free["f"], ready["a"])
                for i in range(2):
                    for n, (f0, fn) in enumerate(FCH):
                        t = mm3(bank["f"][:, i * E:(i + 1) * E], [q[0:fn, n, i * P:(i + 1) * P] for q in (a_h, a_l)],
                                [w[0:fn, n, :] for w in (sd_h, sd_l)], start=n == 0, last=n == len(FCH) - 1)
                last_read["a"] = t
                o_ = ytr[:, k, :].rearrange("p (i e) -> p i e", i=2)
                actq.wait(t)
                t = actq.done(lambda e, o_=o_: e.activation(o_, bank["f"][:].rearrange("p (i e) -> p i e", i=2),
                                                            ACT.Copy))
                free["f"] = t
                sp.wait(t)
                stored["ffn", b, k] = s_ffn[k].start(sp, sum_rows[0][b, :, 2 * k:2 * k + 2, :], o_)
                last_read["ytr"] = [t, stored["ffn", b, k]]
                yield
            dve.wait(ready["keys"])
            span = keys[0:NE, :]
            for r in range(CAP // 8):
                o_ = first[0:NE, 8 * r:8 * r + 8]
                dve.wait(dve.done(lambda e, o_=o_: e.max(o_, span)))
                if r < CAP // 8 - 1:
                    dve.wait(dve.done(lambda e, o_=o_: e.match_replace(span, o_, span, 0.0)))
                if r % 2:
                    yield
            ready["first"] = dve.done(lambda e: e.tensor_copy(keys[0:NE, 0:CAP], first[0:NE, :]))
            dve.wait(ready["first"])

        norm_x()
        split_piece(0, toks[0])
        split_piece(1, toks[1])
        turn_x(0, "s0")
        turn_x(1, "s1")
        split_piece(2, toks[2])
        for n in range(3, len(pieces)):
            split_piece(n, load_piece(n))
        sp.wait(zeroed)
        zero_left = 2 * SUMROWS - NT
        per = 2048 // E * P
        n0 = NT
        while zero_left:
            m = min(per, zero_left)
            if m >= P:
                m = m // P * P
                zt = s_zero.start(sp, sums[n0:n0 + m, :].rearrange("(p r) e -> p (r e)", p=P),
                                  zero_f[:, 0:m // P * E])
            else:
                zt = s_zero.start(sp, sums[n0:n0 + m, :], zero_f[0:m, 0:E])
            n0 += m
            zero_left -= m
        zt = s_zero.start(sp, table[NT:NT + 1, :], zero_f[0:1, 0:ROW])
        for q in (pe, actq, dve, pool):
            q.wait(split[-1], zt, ready["xn"], bq_ready)
        make_k(0, "t0")
        make_v(0, 0, "t1")
        make_v(0, 1, "o")
        make_q(0)

        N = NB * NQ
        pieces_left = []

        def filler(count=1):
            for _ in range(count):
                while pieces_left:
                    try:
                        next(pieces_left[0])
                        break
                    except StopIteration:
                        pieces_left.pop(0)

        def rest_of_kv():
            make_k(1, "f")
            yield
            for s2 in range(TT // 2):
                make_v(1, s2, "f")
                yield
            make_k(2, "f")
            yield
            make_k(3, "f")
            yield

        for n in range(N + 2):
            b, h = n // NQ, n % NQ
            live, prev, pprev = n < N, 0 < n <= N, n >= 2
            if live and h == 0:
                kv_left = rest_of_kv()
            if live:
                scores(n, 3)
            if pprev:
                project_out(n - 2)
                if (n - 2) % NQ == NQ - 1:
                    pieces_left.append(token_layer((n - 2) // NQ))
            if prev:
                turn(n - 1, 3)
            if live:
                normalise(n, 3)
                scores(n, 2)
            if prev:
                turn(n - 1, 2)
                values(n - 1, 3)
            if live:
                normalise(n, 2)
                if h == NQ - 2 and n + 2 < N:
                    x_in = load_x(b + 1, last_read["xio"])
                if h == NQ - 1 and n + 1 < N:
                    norm_x()
                    turn_x(0, "f")
                elif n + 1 < N:
                    make_q(n + 1)
                scores(n, 1)
            if prev:
                turn(n - 1, 1)
                values(n - 1, 2)
            if live:
                normalise(n, 1)
                if h == NQ - 1 and n + 1 < N:
                    turn_x(1, "f")
                scores(n, 0)
            if prev:
                turn(n - 1, 0)
                values(n - 1, 1)
            if live:
                normalise(n, 0)
            if live and h == NQ - 1 and n + 1 < N:
                make_k(0, "f")
                for s2 in range(TT // 2):
                    make_v(0, s2, "f")
                make_q(n + 1)
            if prev:
                values(n - 1, 0)
            if live and h in (0, 1, 2, 4, 6):
                next(kv_left)
            if not (live and h == NQ - 1):
                filler(2)
        while pieces_left:
            filler()

        NP = NE // 2
        everything = [(q.sem, q.count) for q in (pe, dve, actq, pool)]
        s_w = [Slot(sem(f"dma_w{s}")) for s in range(NW)]
        w_read = [None] * NW
        w_in = {}

        def load_expert(e):
            s = e % NW
            if e < NW:
                sp.wait(last_read["xn"] if w_where[s] <= wkv_end else last_read["o"])
            sp.wait(w_read[s])
            for k, w in enumerate((w_gate, w_up)):
                s_w[s].start(sp, w_gu[s][:, :, k * F:(k + 1) * F], w[e].rearrange("(p c) f -> p c f", c=2))
            w_in[e] = s_w[s].start(sp, w_dn[s][0:F2, :, :], w_down[e].rearrange("(p c) h -> p c h", c=2))

        for e in range(NW):
            load_expert(e)
        for q in (pe, dve, actq, pool):
            q.wait(everything)
        stored_all = [stored["x2"], stored["rows"], stored["ffn", NB - 1, 0], stored["ffn", NB - 1, 1], zt]
        for q in (dve, actq, pool):
            q.wait(stored_all)

        def vstep(make):
            dve.wait(dve.done(make))

        key = keys[0:NE, 0:CAP]
        vstep(lambda e: e.tensor_scalar(tok2[0:NE, 0:CAP], key, -1.0, float(NT), ALU.mult, ALU.add))
        vstep(lambda e: e.tensor_copy(tok2[0:NE, CAP:2 * CAP], tok2[0:NE, 0:CAP]))
        vstep(lambda e: e.tensor_scalar(empty[0:NE, :], key, 0.0, None, ALU.is_equal))
        vstep(lambda e: e.tensor_tensor(empty[0:NE, :], empty[0:NE, :], slot_row[0:NE, :], ALU.mult))
        vstep(lambda e: e.tensor_tensor(sct2[0:NE, 0:CAP], tok2[0:NE, 0:CAP], empty[0:NE, :], ALU.add))
        vstep(lambda e: e.tensor_scalar(sct2[0:NE, CAP:2 * CAP], sct2[0:NE, 0:CAP], float(SUMROWS), None, ALU.add))
        t = (dve.sem, dve.count)
        pe.wait(t)
        tr(bank["f"][:, 0:NE], tok2[0:NE, :], ident[0:NE, 0:NE])
        t = tr(bank["f"][:, NE:2 * NE], sct2[0:NE, :], ident[0:NE, 0:NE], last=True)
        dve.wait(t)
        for k, o_ in enumerate((idx_g, idx_s)):
            src = bank["f"][:, k * NE:(k + 1) * NE].rearrange("p (j two) -> p j two", two=2)
            for u in range(2):
                rows_ = slice(u * CAP, (u + 1) * CAP)
                t = dve.done(lambda e, o_=o_, src=src, u=u, rows_=rows_: e.tensor_copy(o_[rows_, :], src[rows_, :, u]))
        idx_ready = t
        pool.wait(idx_ready)
        actq.wait(idx_ready)
        for n in bank:
            free[n] = idx_ready
        s_g = [Slot(sem(f"dma_g{i}")) for i in range(NX)]
        s_s = Slot(sem("dma_s"))
        gathered, scattered = {}, {}
        xg_read, made = {}, {}

        def gather(j):
            s = s_g[j % NX]
            pool.wait(xg_read.get(j - NX))
            s.count += 16
            pool.run(lambda e: e.indirect_dma_start(
                xg[j % NX][:], None, table, bass.IndirectOffsetOnAxis(idx_g[:, j:j + 1].bitcast(U32), 0)
            ).then_inc(s.sem, 16))
            gathered[j] = (s.sem, s.count)

        def scatter(j):
            pool.wait(made["d", j], scattered.get(j - 1))
            s_s.count += 16
            pool.run(lambda e: e.indirect_dma_start(
                sums, bass.IndirectOffsetOnAxis(idx_s[:, j:j + 1].bitcast(U32), 0), dsum[j % 2][:], None,
                compute_op=ALU.add).then_inc(s_s.sem, 16))
            scattered[j] = (s_s.sem, s_s.count)

        def expert_in(j):
            r, bx, bg = j % 2, "y0", f"s{j % 2}"
            pe.wait(gathered[j], free[bx])
            pe.wait(made.get(("xtread", j - 2)))
            src = xg[j % NX][:, 0:E].rearrange("p (m c) -> p m c", c=EC)
            for c in range(EC):
                t = tr(bank[bx][:, c * P:(c + 1) * P], src[:, :, c], ident[:], last=c == EC - 1)
            made["turn", j] = t
            actq.wait(t, made.get(("gu", j - 2)))
            t = actq.done(lambda e: e.activation(xt[r][:, :, :].rearrange("p c n -> p (c n)"),
                                                 bank[bx][:, 0:EC * P], ACT.Copy))
            free[bx] = t
            pe.wait(t, free[bg])
            for u in range(2):
                e_ = 2 * j + u
                pe.wait(w_in[e_])
                for c in range(EC):
                    t = mm(bank[bg][u * CAP:(u + 1) * CAP, 0:2 * F], xt[r][:, c, u * CAP:(u + 1) * CAP],
                           w_gu[e_ % NW][:, c, :], start=c == 0, stop=c == EC - 1, last=c == EC - 1)
            made["gu", j] = t

        def expert_act(j):
            r, bg = j % 2, f"s{j % 2}"
            gate, up = bank[bg][:, 0:F], bank[bg][:, F:2 * F]
            x_, a_ = ex[r][:], ag[r][:]
            actq.wait(made["gu", j], made.get(("act", j - 2)))
            t = actq.done(lambda e: e.activation(x_, gate, ACT.Exp, scale=-1.0))
            dve.wait(t)
            vstep(lambda e: e.tensor_scalar(x_, x_, 1.0, None, ALU.add))
            vstep(lambda e: e.reciprocal(x_, x_))
            vstep(lambda e: e.tensor_tensor(x_, gate, x_, ALU.mult))
            dve.wait(made.get(("at", j - 2)))
            for u in range(2):
                q = slice(u * CAP, (u + 1) * CAP)
                w = xg[j % NX][q, E + 2 * j + u:E + 2 * j + u + 1]
                t = dve.done(lambda e, q=q, w=w: e.scalar_tensor_tensor(
                    out=ag[r][q, :], in0=ex[r][q, :], scalar=w, in1=bank[bg][q, F:2 * F],
                    op0=ALU.mult, op1=ALU.mult))
            free[bg] = made["act", j] = xg_read[j] = t

        def expert_out(j):
            r, ba, bd = j % 2, "y1", f"t{j % 2}"
            pe.wait(made["act", j], free[ba])
            src = ag[r][:].rearrange("p (m c) -> p m c", c=2)
            for c in range(2):
                t = tr(bank[ba][0:F2, c * P:(c + 1) * P], src[:, :, c], ident[:], last=c == 1)
            made["at", j] = t
            actq.wait(t, made.get(("down", j - 2)))
            t = actq.done(lambda e: e.activation(atr[r][0:F2, :, :].rearrange("p c n -> p (c n)"),
                                                 bank[ba][0:F2, 0:2 * P], ACT.Copy))
            free[ba] = t
            pe.wait(t, free[bd])
            for u in range(2):
                e_ = 2 * j + u
                for c in range(2):
                    t = mm(bank[bd][u * CAP:(u + 1) * CAP, 0:E], atr[r][0:F2, c, u * CAP:(u + 1) * CAP],
                           w_dn[e_ % NW][0:F2, c, :], start=c == 0, stop=c == 1, last=c == 1)
                w_read[e_ % NW] = t
            made["down", j] = t
            actq.wait(t, scattered.get(j - 2))
            t = actq.done(lambda e: e.activation(dsum[r][:], bank[bd][:, 0:E], ACT.Copy))
            free[bd] = made["d", j] = t
            for u in range(2):
                if 2 * j + u + NW < NE:
                    load_expert(2 * j + u + NW)

        for j in range(NX - 1):
            gather(j)
        expert_in(0)
        for j in range(NP):
            expert_act(j)
            if j + NX - 1 < NP:
                gather(j + NX - 1)
            if j + 1 < NP:
                expert_in(j + 1)
            expert_out(j)
            scatter(j)

        s_f = [Slot(sem(f"dma_f{i}")) for i in range(NF)]
        s_o = [Slot(sem(f"dma_o{i}")) for i in range(NF)]
        out_rows = out.rearrange("b (i p) e -> b p i e", p=P)
        sp.wait(scattered[NP - 1])
        arrived, out_done = {}, {}

        def load_sums(b):
            i = b % NF
            sp.wait(out_done.get(b - NF))
            s_f[i].start(sp, fa[i][:], sum_rows[0][b])
            s_f[i].start(sp, fb[i][:], sum_rows[1][b])
            arrived[b] = s_f[i].start(sp, fx[i][:], x2_rows[b])

        for b in range(min(NF, NB)):
            load_sums(b)
        for b in range(NB):
            i = b % NF
            dve.wait(arrived[b])
            vstep(lambda e, i=i: e.tensor_tensor(fa[i][:], fa[i][:], fb[i][:], ALU.add))
            statistics([fa[i][:, k, :] for k in range(TT)], fstat, fmv, fnw, 0)
            for k in range(TT):
                t = normed(fa[i][:, k, :], fa[i][:, k, :], fmv, fnw, k)
            dve.wait(t)
            t = dve.done(lambda e, i=i: e.tensor_tensor(fa[i][:], fa[i][:], fx[i][:], ALU.add))
            sp.wait(t)
            out_done[b] = s_o[i].start(sp, out_rows[b], fa[i][:])
            if b + NF < NB:
                load_sums(b + NF)
        sp.wait([out_done[b] for b in range(NB - NF, NB)])

        block = ctx.enter_context(nc.Block())

        @block.sync
        def _(e):
            sp.emit(e)

        @block.gpsimd
        def _(e):
            pool.emit(e)

        @block.scalar
        def _(e):
            actq.emit(e)

        @block.vector
        def _(e):
            dve.emit(e)

        @block.tensor
        def _(e):
            pe.emit(e)


def shape_constants(T, d, NT, cap):
    import numpy as np
    half = T // 2
    pos = np.arange(T, dtype=np.float32)[:, None]
    i = np.arange(0, d, 2, dtype=np.float32)
    inv_freq = np.exp(-(np.log(np.float32(10000.0)) * i / np.float32(d))).astype(np.float32)
    ang = (pos * inv_freq).astype(np.float32)
    pe = np.zeros((T, d), np.float32)
    pe[:, 0::2], pe[:, 1::2] = np.sin(ang), np.cos(ang)
    ident = np.eye(d, dtype=np.float32)
    pe_t = (pe.T * np.float32(float(d) ** -0.25)).astype(np.float32)
    keys = np.broadcast_to(-np.arange(half, dtype=np.float32), (d, half))
    slots = np.broadcast_to(np.arange(cap, dtype=np.float32), (d, cap))
    causal = np.where(np.arange(d)[None, :] > np.arange(d)[:, None], MASKED, 0.0).astype(np.float32)
    return np.ascontiguousarray(np.concatenate([ident, pe_t, keys, slots, causal], axis=1))


def kernel(**inputs):
    import numpy as np
    import concourse.bacc as bacc
    from concourse.bass_utils import run_bass_kernel_spmd

    a = {k: np.asarray(v) for k, v in inputs.items()}
    x = a["L0_attn_x"]
    B, T, E = x.shape
    nq = a["L0_attn_wq"].shape[1] // P
    arrays = {
        "x": x,
        "wq": a["L0_attn_wq"],
        "bqT": a["L0_attn_bq"].reshape(nq, P).T,
        "wkv": a["L0_attn_wkv"],
        "bkvT": a["L0_attn_bkv"].reshape(-1, P).T,
        "wo": a["L0_attn_wo"],
        "gwT": a["L0_ffn_gate_w"].T,
        "w_gate": a["L0_ffn_w_gate"],
        "w_up": a["L0_ffn_w_up"],
        "w_down": a["L0_ffn_w_down"],
        "sgT": a["L0_ffn_sh_gate"].T,
        "suT": a["L0_ffn_sh_up"].T,
        "sdT": a["L0_ffn_sh_down"].T,
        "consts": shape_constants(T, P, B * T, CAP),
    }
    arrays = {k: np.ascontiguousarray(v) for k, v in arrays.items()}
    nc = bacc.Bacc("TRN2", target_bir_lowering=False, num_devices=1)
    args = [nc.dram_tensor(f"in_{k}", v.shape, mybir.dt.from_np(v.dtype), kind="ExternalInput").ap()
            for k, v in arrays.items()]
    out = nc.dram_tensor("out_0", x.shape, F32, kind="ExternalOutput").ap()
    build(nc, *args, out)
    r = run_bass_kernel_spmd(nc, [{f"in_{k}": v for k, v in arrays.items()}], core_ids=[0])
    return r.results[0]["out_0"]
```

```python
from contextlib import ExitStack

import concourse.bass as bass
from concourse import mybir

F32 = mybir.dt.float32
F32R = mybir.dt.float32r
BF16 = mybir.dt.bfloat16
I32 = mybir.dt.int32
U32 = mybir.dt.uint32
ALU = mybir.AluOpType
ACT = mybir.ActivationFunctionType
AX = mybir.AxisListType.X

P = 128
TOP_K = 6
CAP = 64
EPS = 1e-5
MAGIC = 0x5F3759DF
BIG = 3.0e38
MASKED = -1.0e30


class Queue:

    def __init__(self, sem):
        self.sem, self.count, self.steps, self.seen = sem, 0, [], {}

    def wait(self, *tokens):
        for token in tokens:
            if token is None:
                continue
            if isinstance(token, list):
                self.wait(*token)
                continue
            sem, value = token
            if self.seen.get(sem.name, 0) < value:
                self.seen[sem.name] = value
                self.steps.append(lambda e, s=sem, v=value: e.wait_ge(s, v))

    def run(self, make):
        self.steps.append(make)

    def done(self, make):
        self.count += 1
        self.steps.append(lambda e, s=self.sem: make(e).then_inc(s, 1))
        return self.sem, self.count

    def emit(self, engine):
        for step in self.steps:
            step(engine)


class Slot:

    def __init__(self, sem):
        self.sem, self.count = sem, 0

    def start(self, queue, out, in_):
        self.count += 16
        queue.steps.append(lambda e, s=self.sem: e.dma_start(out, in_).then_inc(s, 16))
        return self.sem, self.count


def build(nc, x, wq, bqT, wkv, bkvT, wo, gwT, w_gate, w_up, w_down, sgT, suT, sdT, consts, out):
    NB, T, E = x.shape
    NQ = wq.shape[1] // P
    NG = wkv.shape[1] // (2 * P)
    QPG = NQ // NG
    TT = T // P
    EC = E // P
    NE, _, F = w_gate.shape
    FS = sgT.shape[1]
    NT = NB * T
    FCH = [(f, min(P, FS - f)) for f in range(0, FS, P)]
    HT = T // 2
    F2 = F // 2
    ROW = E + NE
    TRASH = CAP
    SUMROWS = NT + TRASH
    S4 = float(P) ** -0.25
    assert T == 512 and E == 256 and F % 2 == 0 and NE == 64

    table = nc.dram_tensor("token_table", [NT + 1, ROW], F32, kind="Internal").ap()
    x2_dram = nc.dram_tensor("x2_rows", [NT, E], F32, kind="Internal").ap()
    sums = nc.dram_tensor("ffn_sums", [2 * SUMROWS, E], F32, kind="Internal").ap()

    with ExitStack() as ctx:
        def sem(name):
            return ctx.enter_context(nc.semaphore(name))

        at = [0]
        base = nc.sbuf_usable_end - nc.sbuf_bytes_remaining
        at[0] = (base + 31) // 32 * 32

        def place(name, shape, dt):
            size = 4 if dt in (F32, F32R, I32, U32) else 2
            for n in shape[1:]:
                size *= n
            t = nc.alloc_sbuf_tensor_at(name, shape, dt, offset=at[0])
            at[0] += (size + 31) // 32 * 32
            return t

        weights_at = at[0]
        wq_h, wq_l = (place(f"wq_{s}", [P, EC, NQ * P], F32R) for s in "hl")
        wkv_h, wkv_l = (place(f"wkv_{s}", [P, EC, 2 * NG * P], F32R) for s in "hl")
        wkv_end = at[0]
        wo_h, wo_l = (place(f"wo_{s}", [P, NQ, E], F32R) for s in "hl")
        weights_end = at[0]
        sg_h, sg_l = (place(f"sg_{s}", [P, EC, FS], F32R) for s in "hl")
        su_h, su_l = (place(f"su_{s}", [P, EC, FS], F32R) for s in "hl")
        sd_h, sd_l = (place(f"sd_{s}", [P, len(FCH), E], F32R) for s in "hl")
        gw_h, gw_l = (place(f"gw_{s}", [P, EC, NE], F32R) for s in "hl")
        ident = place("ident", [P, P], F32)
        pe_t = place("pe_t", [P, T], F32)
        key_row = place("key_row", [P, HT], F32)
        slot_row = place("slot_row", [P, CAP], F32)
        ident_b = place("ident_b", [P, P], BF16)
        causal_b = place("causal_b", [P, P], BF16)
        bq_s = place("bq_s", [P, NQ], F32)
        bkv_s = place("bkv_s", [P, 2 * NG], F32)
        bk4 = place("bk4", [P, 2 * NG], F32)
        work_at = at[0]
        xn_h, xn_l = (place(f"xn_{s}", [P, EC, T], F32R) for s in "hl")
        k_h, k_l = (place(f"k_{s}", [P, NG, T], F32R) for s in "hl")
        v_h, v_l = (place(f"v_{s}", [P, TT, NG * P], F32R) for s in "hl")
        stage_at = at[0]
        q_sum = place("q_sum", [P, T], F32)
        q_h, q_l = (place(f"q_{s}", [P, 2, T], F32R) for s in "hl")
        tri = [P * (i * (i + 1) // 2) for i in range(TT + 1)]
        inv = [P * (TT * j - j * (j - 1) // 2) for j in range(TT + 1)]
        prob = place("prob", [P, 2, tri[TT]], F32)
        pt_h, pt_l = (place(f"pt_{s}", [P, tri[TT]], F32R) for s in "hl")
        o_h, o_l = (place(f"o_{s}", [P, T], F32R) for s in "hl")
        negmax = place("negmax", [P, 2, TT], F32)
        rsum = place("rsum", [P, 2, TT], F32)
        rinv = place("rinv", [P, 2, TT], F32)
        stage_end = at[0]
        xio = place("xio", [P, TT, E], F32)
        ytr = place("ytr", [P, EC, T], F32)
        rows = place("rows", [P, TT, ROW], F32)
        x2_h, x2_l = (place(f"x2_{s}", [P, EC, HT], F32R) for s in "hl")
        logit = place("logit", [P, 2, NE + 2], F32)
        top8 = place("top8", [P, 2, 8], F32)
        left = place("left", [P, 2, NE + 2], F32)
        mask = place("mask", [P, TT, NE], F32)
        rmax = place("rmax", [P, TT], F32)
        psum_ = place("router_sum", [P, TT], F32)
        pinv = place("router_inv", [P, TT], F32)
        sig = place("sig", [P, HT], F32)
        act = place("act", [P, HT], F32)
        a_h, a_l = (place(f"a_{s}", [P, len(FCH), HT], F32R) for s in "hl")
        keys = place("keys", [P, CAP + T], F32)
        first = place("first", [P, CAP], F32)
        stat = place("stat", [P, TT, 6], F32)
        mv = place("mv", [P, TT, 2], F32)
        nw = place("nw", [P, 4, TT], F32)
        end_at = at[0]
        assert end_at <= nc.sbuf_usable_end, (end_at, nc.sbuf_usable_end)
        at[0] = stage_at
        STG = 2048
        stage = [place(f"stage{i}", [P, STG], F32) for i in range(3)]
        causal_f = place("causal_f", [P, P], F32)
        zero_f = place("zero_f", [P, 2048], F32)
        assert at[0] <= stage_end
        at[0] = weights_at
        NW = 16
        w_gu, w_dn = [], []
        w_where = []
        for s in range(NW):
            w_gu.append(place(f"w_gu{s}", [P, 2, 2 * F], F32))
            w_dn.append(place(f"w_dn{s}", [P, 2, E], F32))
            w_where.append(at[0])
        assert at[0] <= weights_end
        at[0] = stage_at
        NX = 6
        xg = [place(f"xg{i}", [P, ROW], F32) for i in range(NX)]
        xt = [place(f"xt{i}", [P, EC, P], F32) for i in range(2)]
        ex = [place(f"ex{i}", [P, F], F32) for i in range(2)]
        half_w = [place(f"half_w{i}", [P, 1], F32) for i in range(2)]
        ag = [place(f"ag{i}", [P, F], F32) for i in range(2)]
        atr = [place(f"atr{i}", [P, 2, P], F32) for i in range(2)]
        dsum = [place(f"dsum{i}", [P, E], F32) for i in range(2)]
        tok2 = place("tok2", [P, 2 * CAP], F32)
        sct2 = place("sct2", [P, 2 * CAP], F32)
        empty = place("empty", [P, CAP], F32)
        idx_g = place("idx_g", [P, NE // 2], I32)
        idx_s = place("idx_s", [P, NE // 2], I32)
        assert at[0] <= stage_end
        NFB = 4
        fa = [place(f"fa{b}", [P, TT, E], F32) for b in range(NB)]
        fstat = [place(f"fstat{i}", [P, 2 * TT, 6], F32) for i in range(2)]
        fmv = [place(f"fmv{i}", [P, 2 * TT, 2], F32) for i in range(2)]
        fnw = [place(f"fnw{i}", [P, 4, 2 * TT], F32) for i in range(2)]
        fb = [place(f"fb{i}", [P, TT, E], F32) for i in range(2)]
        assert at[0] <= end_at, (at[0], end_at)
        at[0] = work_at
        fb += [place(f"fb{i}", [P, TT, E], F32) for i in range(2, NFB)]
        fx = [place(f"fx{b}", [P, TT, E], F32) for b in range(NB)]
        at[0] = work_at
        x2b_h, x2b_l = (place(f"x2b_{s}", [P, EC, HT], F32R) for s in "hl")
        ab_h, ab_l = (place(f"ab_{s}", [P, len(FCH), HT], F32R) for s in "hl")
        sig_b = place("sig_b", [P, HT], F32)
        act_b = place("act_b", [P, HT], F32)
        assert at[0] <= stage_at

        bank = {n: ctx.enter_context(nc.psum_tensor(f"bank_{n}", [P, 512], F32))
                for n in ("s0", "s1", "t0", "t1", "o", "y0", "y1", "f")}
        free = {n: None for n in bank}

        pe, dve, actq, pool, sp = (Queue(sem(f"{n}_done")) for n in ("pe", "dve", "act", "pool", "sp"))

        def mm(o, l, r, start=False, stop=False, last=False):
            def make(e):
                return e.matmul(o, l, r, start=start, stop=stop, skip_group_check=True)
            return pe.done(make) if last else pe.run(make)

        def mm3(o, l, r, start, last=False):
            mm(o, l[0], r[0], start=start)
            mm(o, l[0], r[1])
            return mm(o, l[1], r[0], stop=True, last=last)

        def tr(o, i, idn, last=False):
            def make(e):
                return e.transpose(o, i, idn)
            return pe.done(make) if last else pe.run(make)

        def f(ap):
            return ap.bitcast(F32)

        s_const, s_zero = Slot(sem("dma_const")), Slot(sem("dma_zero"))
        s_stage = [Slot(sem(f"dma_stage{i}")) for i in range(3)]
        s_x = Slot(sem("dma_x"))
        x_rows = x.rearrange("b (i p) e -> b p i e", p=P)

        def load_x(b, *before):
            sp.wait(*before)
            return s_x.start(sp, xio[:], x_rows[b])

        first_x = load_x(0)
        C = consts
        c0 = 0
        for t, n in ((ident, P), (pe_t, T), (key_row, HT), (slot_row, CAP), (causal_f, P)):
            const_in = s_const.start(sp, t[:, 0:n], C[:, c0:c0 + n])
            c0 += n
        s_const.start(sp, bq_s[:], bqT)
        const_in = s_const.start(sp, bkv_s[:], bkvT)

        pieces = []
        for c in range(EC):
            pieces.append(([(wkv[c * P:(c + 1) * P, :], 0, 2 * NG * P)], P, [
                (0, 2 * NG * P, [t[:, c, :] for t in (wkv_h, wkv_l)], "kv")]))
        for c in range(EC):
            pieces.append(([(wq[c * P:(c + 1) * P, :], 0, NQ * P)], P, [
                (0, NQ * P, [t[:, c, :] for t in (wq_h, wq_l)], S4)]))
        for c in range(2):
            n = NQ // 2
            pieces.append(([(wo[c * n * P:(c + 1) * n * P, :].rearrange("(h p) e -> p h e", p=P), 0, n * E)], P, [
                (0, n * E, [t[:, c * n:(c + 1) * n, :].rearrange("p h e -> p (h e)") for t in (wo_h, wo_l)], 1.0)]))
        pieces.append(([(sgT.rearrange("(c p) f -> p c f", p=P), 0, EC * FS),
                        (suT.rearrange("(c p) f -> p c f", p=P), EC * FS, EC * FS),
                        (gwT.rearrange("(c p) f -> p c f", p=P), 2 * EC * FS, EC * NE)], P, [
            (0, EC * FS, [t[:, :, :].rearrange("p c f -> p (c f)") for t in (sg_h, sg_l)], 1.0),
            (EC * FS, EC * FS, [t[:, :, :].rearrange("p c f -> p (c f)") for t in (su_h, su_l)], 1.0),
            (2 * EC * FS, EC * NE, [t[:, :, :].rearrange("p c f -> p (c f)") for t in (gw_h, gw_l)], 1.0)]))
        whole = [q for q in FCH if q[1] == P]
        pieces.append(([(sdT[0:P * len(whole), :].rearrange("(c p) e -> p c e", p=P), 0, len(whole) * E)], P, [
            (0, len(whole) * E, [t[:, 0:len(whole), :].rearrange("p c e -> p (c e)") for t in (sd_h, sd_l)], 1.0)]))
        if len(whole) < len(FCH):
            r0, rn = FCH[-1]
            pieces.append(([(sdT[r0:r0 + rn, :], 0, E)], rn, [
                (0, E, [t[0:rn, len(whole), :] for t in (sd_h, sd_l)], 1.0)]))

        stage_free = [None] * 3
        split = []

        def load_piece(n):
            sources, rowsn, _ = pieces[n]
            sp.wait(stage_free[n % 3])
            for src, a, w in sources:
                dst = stage[n % 3][0:rowsn, a:a + w]
                if len(src.shape) == 3:
                    dst = dst.rearrange("p (c f) -> p c f", c=src.shape[1])
                tok = s_stage[n % 3].start(sp, dst, src)
            return tok

        def split_piece(n, tok):
            _, rowsn, parts = pieces[n]
            actq.wait(tok)
            dve.wait(tok)
            for a, w, (hi, lo), scale in parts:
                src = stage[n % 3][0:rowsn, a:a + w]
                todo = [(src, hi, lo, scale)]
                if scale == "kv":
                    v = [t.rearrange("p (g two d) -> p g two d", two=2, d=P) for t in (src, hi, lo)]
                    todo = [(*[t[:, :, k, :] for t in v], (S4, 1.0)[k]) for k in range(2)]
                for s_, h_, l_, m_ in todo:
                    t1 = actq.done(lambda e, s_=s_, h_=h_, m_=m_: e.activation(h_, s_, ACT.Copy, scale=m_))
                    dve.wait(t1)
                    t2 = dve.done(lambda e, s_=s_, h_=h_, l_=l_, m_=m_: e.scalar_tensor_tensor(
                        out=l_, in0=s_, scalar=m_, in1=f(h_), op0=ALU.mult, op1=ALU.subtract))
            stage_free[n % 3] = t2
            split.append(t2)

        toks = [load_piece(n) for n in range(3)]
        dve.wait(const_in)
        dve.run(lambda e: e.tensor_copy(ident_b[:], ident[:]))
        dve.run(lambda e: e.tensor_copy(causal_b[:], causal_f[:]))
        dve.run(lambda e: e.memset(logit[:, :, NE:NE + 2], BIG))
        dve.run(lambda e: e.memset(keys[0:NE, 0:CAP], 0.0))
        zeroed = dve.done(lambda e: e.memset(zero_f[:], 0.0))
        dve.run(lambda e: e.tensor_scalar(bk4[:], bkv_s[:], S4, None, ALU.mult))
        dve.wait(zeroed)
        bq_ready = dve.done(lambda e: e.tensor_scalar(bq_s[:], bq_s[:], S4, None, ALU.mult))
        dve.wait(bq_ready)

        def statistics(sources, statt, mvt, nwt, n0):
            n = len(sources)
            for i, s_ in enumerate(sources):
                t = dve.done(lambda e, s_=s_, i=i: e.bn_stats(statt[:, n0 + i, :], s_))
            dve.wait(t)
            for i in range(n):
                t = dve.done(lambda e, i=i: e.bn_aggr(mvt[:, n0 + i, :], statt[:, n0 + i, :]))
            v, y, a = nwt[:, 0, n0:n0 + n], nwt[:, 1, n0:n0 + n], nwt[:, 2, n0:n0 + n]
            var = mvt[:, n0:n0 + n, 1:2].rearrange("p i o -> p (i o)")
            dve.wait(t)
            dve.wait(dve.done(lambda e: e.tensor_scalar(v, var, EPS, None, ALU.add)))
            dve.wait(dve.done(lambda e: e.tensor_scalar(a.bitcast(I32), v.bitcast(I32), 1, None,
                                                        ALU.logical_shift_right)))
            pool.wait(dve.done(lambda e: e.tensor_scalar(y.bitcast(I32), a.bitcast(I32), -1.0, float(MAGIC),
                                                         ALU.mult, ALU.add)))
            for _ in range(3):
                pool.wait(pool.done(lambda e: e.tensor_tensor(a, y, y, ALU.mult)))
                pool.wait(pool.done(lambda e: e.tensor_tensor(a, a, v, ALU.mult)))
                pool.wait(pool.done(lambda e: e.tensor_scalar(a, a, -0.5, 1.5, ALU.mult, ALU.add)))
                t = pool.done(lambda e: e.tensor_tensor(y, a, y, ALU.mult))
                pool.wait(t)
            return t

        def normed(o, s_, mvt, nwt, i):
            return dve.done(lambda e: e.tensor_scalar(o, s_, mvt[:, i, 0:1], nwt[:, 1, i:i + 1],
                                                      ALU.subtract, ALU.mult))

        ready = {}
        last_read = {}
        x_in = {}

        def norm_x(b):
            yield "C"
            dve.wait(x_in[b])
            ready["xstat"] = statistics([xio[:, i, :] for i in range(TT)], stat, mv, nw, 0)
            yield "C"
            dve.wait(ready["xstat"])
            for i in range(TT):
                ready["xnorm"] = normed(xio[:, i, :], xio[:, i, :], mv, nw, i)

        def turn_x(c, bk="f"):
            yield "P"
            pe.wait(ready["xnorm"], free[bk], const_in)
            for i in range(TT):
                t = tr(bank[bk][:, i * P:(i + 1) * P], xio[:, i, c * P:(c + 1) * P], ident[:], last=i == TT - 1)
            last_read["xio"] = t
            yield "C"
            actq.wait(t, last_read.get("xn"))
            t = actq.done(lambda e: e.activation(xn_h[:, c, :], bank[bk][:], ACT.Copy))
            dve.wait(t)
            t = dve.done(lambda e: e.tensor_tensor(xn_l[:, c, :], bank[bk][:], f(xn_h[:, c, :]), ALU.subtract))
            free[bk] = ready["xn"] = t

        def project(bk, hi, lo, col):
            pe.wait(free[bk], ready["xn"])
            for c in range(EC):
                t = mm3(bank[bk][:], [w[:, c, col:col + P] for w in (hi, lo)],
                        [a[:, c, :] for a in (xn_h, xn_l)], start=c == 0, last=c == EC - 1)
            last_read["xn"] = t
            return t

        def with_position(bk, t, bias, h_, l_, before):
            dve.wait(t, last_read.get("q_sum"))
            t = dve.done(lambda e: e.scalar_tensor_tensor(out=q_sum[:], in0=bank[bk][:], scalar=bias,
                                                          in1=pe_t[:], op0=ALU.add, op1=ALU.add))
            free[bk] = t
            actq.wait(t, before)
            t = actq.done(lambda e: e.activation(h_, q_sum[:], ACT.Copy))
            pool.wait(t)
            t = pool.done(lambda e: e.tensor_tensor(l_, q_sum[:], f(h_), ALU.subtract))
            last_read["q_sum"] = t
            return t

        def make_k(g, bk="f"):
            yield "P"
            pe.wait(split[1])
            t = project(bk, wkv_h, wkv_l, 2 * g * P)
            yield "C"
            ready["k", g] = with_position(bk, t, bk4[:, 2 * g:2 * g + 1], k_h[:, g, :], k_l[:, g, :],
                                          last_read.get(("k", g)))

        def make_v(half, s2, bk="f"):
            yield "P"
            pe.wait(free[bk], ready["xn"], split[1])
            ng = NG // 2
            g0 = half * ng
            views = [w[:, :, :].rearrange("p c (g two d) -> p c g two d", two=2, d=P)[:, :, g0:g0 + ng, 1, :]
                     for w in (wkv_h, wkv_l)]
            for k in range(2):
                s = 2 * s2 + k
                o = bank[bk][:, k * ng * P:(k + 1) * ng * P]
                for c in range(EC):
                    t = mm3(o, [a[:, c, s * P:(s + 1) * P] for a in (xn_h, xn_l)],
                            [w[:, c] for w in views], start=c == 0, last=c == EC - 1)
            last_read["xn"] = t
            yield "C"
            src = bank[bk][:].rearrange("p (s n) -> p s n", s=2)
            h_, l_ = (v[:, 2 * s2:2 * s2 + 2, g0 * P:(g0 + ng) * P] for v in (v_h, v_l))
            actq.wait(t, last_read.get(("v", half)))
            t = actq.done(lambda e: e.activation(h_, src, ACT.Copy))
            dve.wait(t)
            t = dve.done(lambda e: e.tensor_tensor(l_, src, f(h_), ALU.subtract))
            free[bk] = ready["v", half] = t

        def make_q(n, bk="f"):
            h = n % NQ
            yield "P"
            pe.wait(split[3])
            t = project(bk, wq_h, wq_l, h * P)
            yield "C"
            ready["q", n] = with_position(bk, t, bq_s[:, h:h + 1], q_h[:, n % 2, :], q_l[:, n % 2, :],
                                          last_read.get(("q", n - 2)))

        def at_once(gen):
            for _ in gen:
                pass

        def scores(n, i):
            h, r = n % NQ, n % 2
            g, w, bk = h // QPG, (i + 1) * P, f"s{i % 2}"
            pe.wait(free[bk], ready["q", n], ready["k", g])
            mm(bank[bk][:, i * P:w], ident_b[:], causal_b[:], start=True)
            t = mm3(bank[bk][:, 0:w], [q[:, r, i * P:(i + 1) * P] for q in (q_h, q_l)],
                    [k[:, g, 0:w] for k in (k_h, k_l)], start=False, last=True)
            last_read["q", n] = last_read["k", g] = t
            dve.wait(t, ready.get(("exp", n - 2, i)))
            ready["max", n, i] = dve.done(lambda e: e.reduce_max(negmax[:, r, i:i + 1], bank[bk][:, 0:w], AX,
                                                                 negate=True))

        def exponentials(n, i):
            r, w, bk = n % 2, (i + 1) * P, f"s{i % 2}"
            actq.wait(ready["max", n, i], ready.get(("turned", n - 2)), ready.get(("rinv", n - 2, i)))
            t = actq.done(lambda e: e.activation(prob[:, r, tri[i]:tri[i + 1]], bank[bk][:, 0:w], ACT.Exp,
                                                 bias=negmax[:, r, i:i + 1], accum_out=rsum[:, r, i:i + 1]))
            free[bk] = ready["exp", n, i] = t

        def normalise(n, i):
            r = n % 2
            dve.wait(ready["exp", n, i], ready.get(("normal", n - 2, i)))
            t = dve.done(lambda e: e.reciprocal(rinv[:, r, i:i + 1], rsum[:, r, i:i + 1]))
            ready["rinv", n, i] = t
            pool.wait(t)
            p_ = prob[:, r, tri[i]:tri[i + 1]]
            w = (i + 1) * P
            ready["normal", n, i] = pool.done(lambda e: e.tensor_tensor(
                p_, p_, rinv[:, r, i:i + 1].to_broadcast([P, w]), ALU.mult))

        def turn(n, j):
            r, bk = n % 2, f"t{j % 2}"
            pe.wait(free[bk], [ready["normal", n, i] for i in range(j, TT)])
            for i in range(j, TT):
                t = tr(bank[bk][:, (i - j) * P:(i - j + 1) * P],
                       prob[:, r, tri[i] + j * P:tri[i] + (j + 1) * P], ident[:], last=i == TT - 1)
            ready["turn", n, j] = t
            if j == 0:
                ready["turned", n] = t

        def turned_high(n, j):
            bk, w, h_ = f"t{j % 2}", (TT - j) * P, pt_h[:, inv[j]:inv[j + 1]]
            actq.wait(ready["turn", n, j], last_read.get(("pt", j)))
            ready["pth", n, j] = actq.done(lambda e: e.activation(h_, bank[bk][:, 0:w], ACT.Copy))

        def turned_low(n, j):
            bk, w = f"t{j % 2}", (TT - j) * P
            h_, l_ = (q[:, inv[j]:inv[j + 1]] for q in (pt_h, pt_l))
            dve.wait(ready["pth", n, j])
            t = dve.done(lambda e: e.tensor_tensor(l_, bank[bk][:, 0:w], f(h_), ALU.subtract))
            free[bk] = ready["pt", n, j] = t

        def values(n, j):
            g = n % NQ // QPG
            pe.wait(ready["pt", n, j], ready["v", g // (NG // 2)])
            if j == TT - 1:
                pe.wait(free["o"])
            t = mm3(bank["o"][:, j * P:T], [v[:, j, g * P:(g + 1) * P] for v in (v_h, v_l)],
                    [q[:, inv[j]:inv[j + 1]] for q in (pt_h, pt_l)], start=j == TT - 1, last=True)
            last_read["pt", j] = last_read["v", g // (NG // 2)] = t
            ready["o_bank"] = t

        def output_high(n):
            g = n % NQ // QPG
            bias = bkv_s[:, 2 * g + 1:2 * g + 2]
            actq.wait(ready["o_bank"], last_read.get("o"))
            ready["oh"] = actq.done(lambda e: e.activation(o_h[:], bank["o"][:], ACT.Identity, bias=bias))

        def output_low(n):
            g = n % NQ // QPG
            bias = bkv_s[:, 2 * g + 1:2 * g + 2]
            dve.wait(ready["oh"])
            free["o"] = ready["o"] = dve.done(lambda e: e.scalar_tensor_tensor(
                out=o_l[:], in0=bank["o"][:], scalar=bias, in1=f(o_h[:]), op0=ALU.add, op1=ALU.subtract))

        def project_out(n):
            h = n % NQ
            pe.wait(ready["o"], split[5])
            if h == 0:
                pe.wait(free["y0"], free["y1"])
            for c in range(EC):
                t = mm3(bank[f"y{c}"][:], [w[:, h, c * P:(c + 1) * P] for w in (wo_h, wo_l)],
                        [o_h[:], o_l[:]], start=h == 0, last=c == EC - 1)
            last_read["o"] = t
            if h == NQ - 1:
                actq.wait(t, last_read.get("ytr"))
                dve.wait(t, last_read.get("ytr"))
                free["y0"] = actq.done(lambda e: e.activation(ytr[:, 0, :], bank["y0"][:], ACT.Copy))
                free["y1"] = dve.done(lambda e: e.tensor_copy(ytr[:, 1, :], bank["y1"][:]))
                ready["ytr"] = [free["y0"], free["y1"]]

        s_x2, s_rows, s_ffn = Slot(sem("dma_x2")), Slot(sem("dma_rows")), [Slot(sem(f"dma_ffn{k}")) for k in range(2)]
        stored = {}
        x2_rows = x2_dram.rearrange("(b i p) e -> b p i e", p=P, i=TT)
        table_rows = table[0:NT, :].rearrange("(b i p) e -> b p i e", p=P, i=TT)
        sum_rows = [sums[a * SUMROWS:a * SUMROWS + NT, :].rearrange("(b i p) e -> b p i e", p=P, i=TT)
                    for a in range(2)]
        pick_of = {}

        def pick(b):
            span = keys[0:NE, :]
            for r in range(CAP // 8):
                yield "C"
                o_ = first[0:NE, 8 * r:8 * r + 8]
                dve.wait(ready["keys"])
                dve.wait(dve.done(lambda e, o_=o_: e.max(o_, span)))
                if r < CAP // 8 - 1:
                    dve.wait(dve.done(lambda e, o_=o_: e.match_replace(span, o_, span, 0.0)))
            dve.wait(dve.done(lambda e: e.tensor_copy(keys[0:NE, 0:CAP], first[0:NE, :])))

        def token_norms(b, banks):
            yield "C"
            x_again = load_x(b, last_read["xio"])
            for k in range(2):
                yield "P"
                bk = banks[k]
                bf = bank[bk]
                pe.wait(free[bk], ready["ytr"])
                for i in range(2):
                    for c in range(EC):
                        t = tr(bf[:, i * E + c * P:i * E + (c + 1) * P],
                               ytr[:, c, (2 * k + i) * P:(2 * k + i + 1) * P], ident[:],
                               last=(i, c) == (1, EC - 1))
                last_read["ytr"] = t
                yield "C"
                actq.wait(t, stored.get("rows"))
                t = free[bk] = actq.done(lambda e, k=k, bf=bf: e.activation(
                    rows[:, 2 * k:2 * k + 2, 0:E], bf[:].rearrange("p (i e) -> p i e", i=2), ACT.Copy))
            yield "C"
            dve.wait(t)
            t = statistics([rows[:, i, 0:E] for i in range(TT)], stat, mv, nw, 0)
            yield "C"
            dve.wait(t)
            for i in range(TT):
                t = normed(rows[:, i, 0:E], rows[:, i, 0:E], mv, nw, i)
            pool.wait(t, x_again)
            t = pool.done(lambda e: e.tensor_tensor(xio[:], xio[:], rows[:, :, 0:E], ALU.add))
            yield "C"
            yield "C"
            dve.wait(t)
            t2 = statistics([xio[:, i, :] for i in range(TT)], stat, mv, nw, 0)
            sp.wait(t)
            stored["x2"] = s_x2.start(sp, x2_rows[b], xio[:])
            yield "C"
            dve.wait(t2)
            for i in range(TT):
                t = normed(rows[:, i, 0:E], xio[:, i, :], mv, nw, i)
            ready["ln2"] = t
            last_read["xio"] = [stored["x2"], t]

        lanes = [(x2_h, x2_l, a_h, a_l, sig, act), (x2b_h, x2b_l, ab_h, ab_l, sig_b, act_b)]

        def route(b, k, bk, lane):
            bf = bank[bk]
            x2h, x2l = lanes[lane][0:2]
            k2 = slice(2 * k, 2 * k + 2)
            yield "P"
            pe.wait(ready["ln2"], free[bk])
            for c in range(EC):
                for i in range(2):
                    t = tr(bf[:, c * HT + i * P:c * HT + (i + 1) * P],
                           rows[:, 2 * k + i, c * P:(c + 1) * P], ident[:], last=(c, i) == (EC - 1, 1))
            yield "C"
            src = bf[:].rearrange("p (c t) -> p c t", c=EC)
            actq.wait(t, last_read.get(("x2", lane)))
            t = actq.done(lambda e, src=src: e.activation(x2h[:], src, ACT.Copy))
            dve.wait(t)
            t = dve.done(lambda e, src=src: e.tensor_tensor(x2l[:], src, f(x2h[:]), ALU.subtract))
            free[bk] = ready["x2", lane] = t
            yield "P"
            pe.wait(ready["x2", lane], free[bk], split[6])
            for i in range(2):
                for c in range(EC):
                    t = mm3(bf[:, i * NE:(i + 1) * NE],
                            [a[:, c, i * P:(i + 1) * P] for a in (x2h, x2l)],
                            [w[:, c, :] for w in (gw_h, gw_l)], start=c == 0, last=c == EC - 1)
            yield "C"
            dve.wait(t, ready.get("router_exp"))
            t = dve.done(lambda e: e.tensor_copy(logit[:, :, 0:NE], bf[:, 0:2 * NE].rearrange(
                "p (i n) -> p i n", i=2)))
            free[bk] = t
            dve.wait(t)
            for i in range(2):
                t = dve.done(lambda e, i=i: e.max(top8[:, i, :], logit[:, i, :]))
            dve.wait(t)
            t2 = dve.done(lambda e: e.tensor_scalar(rmax[:, k2], top8[:, :, 2:3].rearrange("p i o -> p (i o)"),
                                                    -1.0, None, ALU.mult))
            for i in range(2):
                t = dve.done(lambda e, i=i: e.match_replace(left[:, i, :], top8[:, i, :], logit[:, i, :], -BIG))
            dve.wait(t, last_read.get(("mask", k)))
            ready["mask", k] = dve.done(lambda e: e.tensor_scalar(mask[:, k2, :], left[:, :, 0:NE], -BIG, None,
                                                               ALU.is_equal))
            actq.wait(t2)
            for i in range(2):
                o_ = rows[:, 2 * k + i, E:ROW]
                t = actq.done(lambda e, i=i, o_=o_: e.activation(o_, logit[:, i, 0:NE], ACT.Exp,
                                                                 bias=rmax[:, 2 * k + i:2 * k + i + 1],
                                                                 accum_out=psum_[:, 2 * k + i:2 * k + i + 1]))
            ready["router_exp"] = t
            yield "P"
            pe.wait(ready["mask", k], free[bk])
            for i in range(2):
                t = tr(bf[0:NE, i * P:(i + 1) * P], mask[:, 2 * k + i, :], ident[:], last=i == 1)
            last_read["mask", k] = t
            yield "C"
            if k == 0 and b:
                at_once(pick_of.pop(b - 1, ()))
            off = float(NT - b * T - k * HT)
            o_ = keys[0:NE, CAP + k * HT:CAP + (k + 1) * HT]
            dve.wait(t)
            t = dve.done(lambda e, off=off, o_=o_: e.scalar_tensor_tensor(
                out=o_, in0=key_row[0:NE, :], scalar=off, in1=bf[0:NE, 0:HT],
                op0=ALU.add, op1=ALU.mult))
            free[bk] = ready["keys"] = t
            if k == 1:
                pick_of[b] = pick(b)
            dve.wait(ready["router_exp"])
            t = dve.done(lambda e: e.reciprocal(pinv[:, k2], psum_[:, k2]))
            dve.wait(t)
            for i in range(2):
                o_ = rows[:, 2 * k + i, E:ROW]
                t = dve.done(lambda e, i=i, o_=o_: e.tensor_scalar(o_, o_, pinv[:, 2 * k + i:2 * k + i + 1], None, ALU.mult))
            if k == 1:
                sp.wait(t)
                stored["rows"] = s_rows.start(sp, table_rows[b], rows[:])

        def shared_expert(b, k, bk, lane):
            bf = bank[bk]
            x2h, x2l, ah, al, sg_, ac_ = lanes[lane]
            for n, (f0, fn) in enumerate(FCH):
                yield "P"
                pe.wait(free[bk], ready["x2", lane], split[-1])
                for u, (hi, lo) in enumerate(((sg_h, sg_l), (su_h, su_l))):
                    for c in range(EC):
                        t = mm3(bf[0:fn, u * HT:(u + 1) * HT], [w[:, c, f0:f0 + fn] for w in (hi, lo)],
                                [a[:, c, :] for a in (x2h, x2l)], start=c == 0, last=c == EC - 1)
                last_read["x2", lane] = t
                yield "C"
                gate, up = bf[0:fn, 0:HT], bf[0:fn, HT:2 * HT]
                s_, a_ = sg_[0:fn, :], ac_[0:fn, :]
                actq.wait(t, ready.get(("act", lane)))
                t = actq.done(lambda e, s_=s_, gate=gate: e.activation(s_, gate, ACT.Tanh, scale=0.5))
                dve.wait(t)
                t = dve.done(lambda e, s_=s_, gate=gate: e.scalar_tensor_tensor(
                    out=s_, in0=s_, scalar=1.0, in1=gate, op0=ALU.add, op1=ALU.mult))
                dve.wait(t, last_read.get(("act", lane)))
                t = dve.done(lambda e, s_=s_, a_=a_, up=up: e.scalar_tensor_tensor(
                    out=a_, in0=s_, scalar=0.5, in1=up, op0=ALU.mult, op1=ALU.mult))
                free[bk] = ready["act", lane] = t
                h_, l_ = (q[0:fn, n, :] for q in (ah, al))
                actq.wait(t, last_read.get(("a", lane)))
                t = actq.done(lambda e, h_=h_, a_=a_: e.activation(h_, a_, ACT.Copy))
                pool.wait(t)
                t = pool.done(lambda e, l_=l_, h_=h_, a_=a_: e.tensor_tensor(l_, a_, f(h_), ALU.subtract))
                last_read["act", lane] = t
                ready["a", lane] = t
            yield "P"
            pe.wait(free[bk], ready["a", lane])
            for i in range(2):
                for n, (f0, fn) in enumerate(FCH):
                    t = mm3(bf[:, i * E:(i + 1) * E], [q[0:fn, n, i * P:(i + 1) * P] for q in (ah, al)],
                            [w[0:fn, n, :] for w in (sd_h, sd_l)], start=n == 0, last=n == len(FCH) - 1)
            last_read["a", lane] = t
            yield "C"
            o_ = ytr[:, k, :].rearrange("p (i e) -> p i e", i=2)
            actq.wait(t)
            t = actq.done(lambda e, o_=o_: e.activation(o_, bf[:].rearrange("p (i e) -> p i e", i=2), ACT.Copy))
            free[bk] = t
            sp.wait(t)
            stored["ffn", b, k] = s_ffn[k].start(sp, sum_rows[0][b, :, 2 * k:2 * k + 2, :], o_)
            last_read["ytr"] = [t, stored["ffn", b, k]]

        def token_layer(b):
            yield from token_norms(b, "ff")
            for k in range(2):
                yield from route(b, k, "f", 0)
                yield from shared_expert(b, k, "f", 0)

        x_in[0] = first_x
        at_once(norm_x(0))
        split_piece(0, toks[0])
        split_piece(1, toks[1])
        at_once(turn_x(0, "s0"))
        at_once(turn_x(1, "s1"))
        split_piece(2, toks[2])
        for n in range(3, len(pieces)):
            split_piece(n, load_piece(n))
        sp.wait(zeroed)
        zero_left = 2 * SUMROWS - NT
        per = 2048 // E * P
        n0 = NT
        while zero_left:
            m = min(per, zero_left)
            if m >= P:
                m = m // P * P
                zt = s_zero.start(sp, sums[n0:n0 + m, :].rearrange("(p r) e -> p (r e)", p=P),
                                  zero_f[:, 0:m // P * E])
            else:
                zt = s_zero.start(sp, sums[n0:n0 + m, :], zero_f[0:m, 0:E])
            n0 += m
            zero_left -= m
        zt = s_zero.start(sp, table[NT:NT + 1, :], zero_f[0:1, 0:ROW])
        for q in (pe, actq, dve, pool):
            q.wait(split[-1], zt, ready["xn"], bq_ready)
        at_once(make_k(0, "t0"))
        at_once(make_q(0))

        N = NB * NQ

        class Behind:

            def __init__(self, *gens):
                self.gens, self.tag = list(gens), None
                self.step(first=True)

            def step(self, first=False):
                while self.gens:
                    try:
                        self.tag = next(self.gens[0])
                        return
                    except StopIteration:
                        self.gens.pop(0)
                self.tag = None

        tasks = {}
        holding = [None]

        def later(kind, *gens):
            if kind in tasks:
                tasks[kind].gens += gens
            else:
                tasks[kind] = Behind(*gens)

        def part(kinds, tags):
            for kind in ([holding[0]] if holding[0] else kinds):
                task = tasks.get(kind)
                if task and task.tag in tags:
                    holding[0] = kind if task.tag == "P" else None
                    task.step()
                    if task.tag is None:
                        del tasks[kind]
                    return True
            return False

        kv_at = {0: [(make_v, 0, 0), (make_v, 0, 1)], 2: [(make_k, 1)], 4: [(make_v, 1, 0)],
                 5: [(make_v, 1, 1)], 6: [(make_k, 2)], 9: [(make_k, 3)]}
        def normalised(n, ph):
            if ph and n < N:
                normalise(n, TT - ph)
            elif not ph and 0 < n <= N:
                normalise(n - 1, 0)

        turns = []
        q_parts = None
        output = None
        behind = ["kv", "xnorm", "tokens"]
        for n in range(N + 3):
            b, h = n // NQ, n % NQ
            live = n < N
            if live:
                if h in kv_at:
                    later("kv", *(m(*a) for m, *a in kv_at[h]))
                if b + 1 < NB:
                    if h == NQ - 4:
                        x_in[b + 1] = load_x(b + 1, last_read["xio"])
                        later("xnorm", norm_x(b + 1))
                    if h == NQ - 2:
                        later("kv", turn_x(0), turn_x(1))
                    if h == NQ - 1:
                        later("kv", make_k(0))
            for ph in range(TT):
                i = TT - 1 - ph
                turned = turns[-1] if turns else None
                if live:
                    scores(n, i)
                if ph == 3 and output is not None:
                    output_high(output)
                if turned:
                    turned_high(*turned)
                if live:
                    exponentials(n, i)
                if ph == 3 and output is not None:
                    output_low(output)
                if turned:
                    turned_low(*turned)
                normalised(n, ph)
                if ph == 2 and q_parts:
                    at_once(q_parts)
                    q_parts = None
                if ph == 0 and output is not None:
                    project_out(output)
                    if output % NQ == NQ - 1:
                        if output < N - 1:
                            later("tokens", token_layer(output // NQ))
                    output = None
                turns.append((n - 1, i) if 0 < n <= N else None)
                if turns[-1]:
                    turn(n - 1, i)
                if len(turns) > 3 and turns[-4]:
                    values(*turns[-4])
                    if turns[-4][1] == 0:
                        output = turns[-4][0]
                if ph == 0:
                    part(behind, "C")
                elif ph == 1:
                    if live and n + 1 < N:
                        q_parts = make_q(n + 1)
                        next(q_parts)
                        next(q_parts)
                    else:
                        part(behind, "C")
                elif ph == 2:
                    part(behind, "PC")
                else:
                    part(behind, "PC")
                    if not holding[0]:
                        part(behind, "PC")
                if ph in (1, 2) and pick_of:
                    m = min(pick_of)
                    if next(pick_of[m], None) is None:
                        del pick_of[m]
        while tasks:
            if not part(["kv", "xnorm", "tokens"], "PC"):
                break
        for m in list(pick_of):
            at_once(pick_of.pop(m))
        heads_through = [(q.sem, q.count) for q in (pe, dve, actq, pool)]
        for q in (pe, dve, actq, pool):
            q.wait(heads_through)

        NP = NE // 2
        s_w = [Slot(sem(f"dma_w{s}")) for s in range(NW)]
        w_read = [None] * NW
        w_in = {}

        def load_expert(e):
            s = e % NW
            if e < NW:
                sp.wait(last_read["xn"] if w_where[s] <= wkv_end else last_read["o"])
            sp.wait(w_read[s])
            for k, w in enumerate((w_gate, w_up)):
                s_w[s].start(sp, w_gu[s][:, :, k * F:(k + 1) * F], w[e].rearrange("(p c) f -> p c f", c=2))
            w_in[e] = s_w[s].start(sp, w_dn[s][0:F2, :, :], w_down[e].rearrange("(p c) h -> p c h", c=2))

        last = NB - 1
        norms = token_norms(last, ("s0", "t0"))
        next(norms)
        next(norms)
        for e in range(NW):
            load_expert(e)
        at_once(norms)
        for _ in zip(route(last, 0, "s0", 0), route(last, 1, "t0", 1), strict=True):
            pass
        picks = pick_of.pop(last)
        for _ in zip(shared_expert(last, 0, "s1", 0), shared_expert(last, 1, "t1", 1), strict=True):
            next(picks, None)
        at_once(picks)
        shared_through = [(q.sem, q.count) for q in (pe, dve, actq, pool)]
        stored_rows = [stored["rows"], zt]
        stored_ffn = [stored["ffn", last, 0], stored["ffn", last, 1], zt]

        key = keys[0:NE, 0:CAP]
        dve.wait((dve.sem, dve.count))
        for u in range(2):
            t = dve.done(lambda e, u=u: e.tensor_scalar(tok2[0:NE, u * CAP:(u + 1) * CAP], key, -1.0, float(NT),
                                                        ALU.mult, ALU.add))
        t = dve.done(lambda e: e.scalar_tensor_tensor(out=empty[0:NE, :], in0=key, scalar=0.0,
                                                      in1=slot_row[0:NE, :], op0=ALU.is_equal, op1=ALU.mult))
        dve.wait(t)
        for u in range(2):
            t = dve.done(lambda e, u=u: e.scalar_tensor_tensor(
                out=sct2[0:NE, u * CAP:(u + 1) * CAP], in0=tok2[0:NE, 0:CAP], scalar=float(u * SUMROWS),
                in1=empty[0:NE, :], op0=ALU.add, op1=ALU.add))
        pe.wait(t, free["f"])
        tr(bank["f"][:, 0:NE], tok2[0:NE, :], ident[0:NE, 0:NE])
        t = tr(bank["f"][:, NE:2 * NE], sct2[0:NE, :], ident[0:NE, 0:NE], last=True)
        dve.wait(t)
        for k, o_ in enumerate((idx_g, idx_s)):
            src = bank["f"][:, k * NE:(k + 1) * NE].rearrange("p (j two) -> p j two", two=2)
            for u in range(2):
                rows_ = slice(u * CAP, (u + 1) * CAP)
                t = dve.done(lambda e, o_=o_, src=src, u=u, rows_=rows_: e.tensor_copy(o_[rows_, :], src[rows_, :, u]))
        free["f"] = t
        pool.wait(t, stored_rows)

        def vstep(make):
            dve.wait(dve.done(make))

        s_g = [Slot(sem(f"dma_g{i}")) for i in range(NX)]
        s_s = Slot(sem("dma_s"))
        s_x2in = Slot(sem("dma_x2_in"))
        gathered, scattered = {}, {}
        xg_read, made = {}, {}

        def gather(j):
            s = s_g[j % NX]
            pool.wait(xg_read.get(j - NX))
            s.count += 16
            pool.run(lambda e: e.indirect_dma_start(
                xg[j % NX][:], None, table, bass.IndirectOffsetOnAxis(idx_g[:, j:j + 1].bitcast(U32), 0)
            ).then_inc(s.sem, 16))
            gathered[j] = (s.sem, s.count)

        def scatter(j):
            pool.wait(made["d", j], stored_ffn, scattered.get(j - 1))
            s_s.count += 16
            pool.run(lambda e: e.indirect_dma_start(
                sums, bass.IndirectOffsetOnAxis(idx_s[:, j:j + 1].bitcast(U32), 0), dsum[j % 2][:], None,
                compute_op=ALU.add).then_inc(s_s.sem, 16))
            scattered[j] = (s_s.sem, s_s.count)

        def expert_turn(j):
            r, bx = j % 2, f"y{j % 2}"
            pe.wait(gathered[j], free[bx])
            src = xg[j % NX][:, 0:E].rearrange("p (m c) -> p m c", c=EC)
            for c in range(EC):
                t = tr(bank[bx][:, c * P:(c + 1) * P], src[:, :, c], ident[:], last=c == EC - 1)
            actq.wait(t, made.get(("gu", j - 2)))
            t = actq.done(lambda e: e.activation(xt[r][:, :, :].rearrange("p c n -> p (c n)"),
                                                 bank[bx][:, 0:EC * P], ACT.Copy))
            free[bx] = made["xt", j] = t

        def expert_in(j):
            r, bg = j % 2, f"s{j % 2}"
            pe.wait(made["xt", j], free[bg])
            for u in range(2):
                e_ = 2 * j + u
                pe.wait(w_in[e_])
                for c in range(EC):
                    t = mm(bank[bg][u * CAP:(u + 1) * CAP, 0:2 * F], xt[r][:, c, u * CAP:(u + 1) * CAP],
                           w_gu[e_ % NW][:, c, :], start=c == 0, stop=c == EC - 1, last=c == EC - 1)
            made["gu", j] = t

        def expert_act(j):
            r, bg = j % 2, f"s{j % 2}"
            gate, up = bank[bg][:, 0:F], bank[bg][:, F:2 * F]
            x_, a_ = ex[r][:], ag[r][:]
            actq.wait(made["gu", j], made.get(("act", j - 2)))
            t = actq.done(lambda e: e.activation(x_, gate, ACT.Tanh, scale=0.5))
            dve.wait(gathered[j], made.get(("act", j - 2)))
            for u in range(2):
                q = slice(u * CAP, (u + 1) * CAP)
                t2 = dve.done(lambda e, q=q, u=u: e.tensor_scalar(
                    half_w[r][q, :], xg[j % NX][q, E + 2 * j + u:E + 2 * j + u + 1], 0.5, None, ALU.mult))
            xg_read[j] = t2
            dve.wait(t, t2)
            vstep(lambda e: e.scalar_tensor_tensor(out=x_, in0=x_, scalar=1.0, in1=gate, op0=ALU.add, op1=ALU.mult))
            dve.wait(made.get(("at", j - 2)))
            t = dve.done(lambda e: e.scalar_tensor_tensor(out=a_, in0=x_, scalar=half_w[r][:], in1=up,
                                                          op0=ALU.mult, op1=ALU.mult))
            free[bg] = made["act", j] = t

        def activations_turn(j):
            r, ba = j % 2, "of"[j % 2]
            pe.wait(made["act", j], free[ba])
            src = ag[r][:].rearrange("p (m c) -> p m c", c=2)
            for c in range(2):
                t = tr(bank[ba][0:F2, c * P:(c + 1) * P], src[:, :, c], ident[:], last=c == 1)
            made["at", j] = t
            actq.wait(t, made.get(("down", j - 2)))
            t = actq.done(lambda e: e.activation(atr[r][0:F2, :, :].rearrange("p c n -> p (c n)"),
                                                 bank[ba][0:F2, 0:2 * P], ACT.Copy))
            free[ba] = made["atr", j] = t

        def expert_out(j):
            r, bd = j % 2, f"t{j % 2}"
            pe.wait(made["atr", j], free[bd])
            for u in range(2):
                e_ = 2 * j + u
                for c in range(2):
                    t = mm(bank[bd][u * CAP:(u + 1) * CAP, 0:E], atr[r][0:F2, c, u * CAP:(u + 1) * CAP],
                           w_dn[e_ % NW][0:F2, c, :], start=c == 0, stop=c == 1, last=c == 1)
                w_read[e_ % NW] = t
            made["down", j] = t
            actq.wait(t, scattered.get(j - 2))
            t = actq.done(lambda e: e.activation(dsum[r][:], bank[bd][:, 0:E], ACT.Copy))
            free[bd] = made["d", j] = t
            for u in range(2):
                if 2 * j + u + NW < NE:
                    load_expert(2 * j + u + NW)

        for j in range(NX - 1):
            gather(j)
        expert_turn(0)
        expert_turn(1)
        expert_in(0)
        expert_act(0)
        for j in range(NP):
            if j + 2 < NP:
                expert_turn(j + 2)
            activations_turn(j)
            if j + 1 < NP:
                expert_in(j + 1)
                expert_act(j + 1)
            expert_out(j)
            if j + NX - 1 < NP:
                gather(j + NX - 1)
            scatter(j)
            if j % 2 and j // 2 < NB:
                b = j // 2
                sp.wait(shared_through, stored["x2"], stored_ffn)
                x2_in = s_x2in.start(sp, fx[b][:], x2_rows[b])

        s_f = [Slot(sem(f"dma_f{i}")) for i in range(NB)]
        s_o = Slot(sem("dma_out"))
        out_rows = out.rearrange("b (i p) e -> b p i e", p=P)
        sp.wait(scattered[NP - 1])
        arrived, summed, added = {}, {}, {}

        def load_sums(b):
            sp.wait(summed.get(b - NFB))
            s_f[b].start(sp, fa[b][:], sum_rows[0][b])
            arrived[b] = s_f[b].start(sp, fb[b % NFB][:], sum_rows[1][b])

        def add_sums(b):
            pool.wait(arrived[b])
            dve.wait(arrived[b])
            summed[b] = [q.done(lambda e, k=k: e.tensor_tensor(fa[b][:, k, :], fa[b][:, k, :],
                                                               fb[b % NFB][:, k, :], ALU.add))
                         for q, k in ((pool, slice(0, TT - 1)), (dve, slice(TT - 1, TT)))]

        def pair_statistics(p):
            dve.wait(summed[2 * p + 1])
            mean = fmv[p % 2][:, :, 0:1].rearrange("p i o -> p (i o)")
            inv_, bias = fnw[p % 2][:, 1, :], fnw[p % 2][:, 3, :]
            dve.wait(added.get(("norm", 2 * p - 3)))
            pool.wait(added.get(("norm", 2 * p - 3)))
            pool.wait(statistics([fa[b][:, k, :] for b in (2 * p, 2 * p + 1) for k in range(TT)],
                                 fstat[p % 2], fmv[p % 2], fnw[p % 2], 0))
            pool.wait(pool.done(lambda e: e.tensor_tensor(bias, mean, inv_, ALU.mult)))
            added["bias", p] = pool.done(lambda e: e.tensor_scalar(bias, bias, -1.0, None, ALU.mult))

        def normalise_out(b):
            nw_, k0 = fnw[b // 2 % 2], b % 2 * TT
            actq.wait(added["bias", b // 2])
            for k in range(TT):
                t = actq.done(lambda e, k=k: e.activation(fa[b][:, k, :], fa[b][:, k, :], ACT.Identity,
                                                          scale=nw_[:, 1, k0 + k:k0 + k + 1],
                                                          bias=nw_[:, 3, k0 + k:k0 + k + 1]))
            added["norm", b] = t

        def residual_out(b):
            dve.wait(added["norm", b], x2_in)
            t = dve.done(lambda e: e.tensor_tensor(fa[b][:], fa[b][:], fx[b][:], ALU.add))
            sp.wait(t)
            added["out"] = s_o.start(sp, out_rows[b], fa[b][:])

        for b in range(min(NFB, NB)):
            load_sums(b)
        add_sums(0)
        add_sums(1)
        for p in range(NB // 2):
            for b in (2 * p + 2, 2 * p + 3):
                if b < NB:
                    add_sums(b)
                if b - 2 + NFB < NB:
                    load_sums(b - 2 + NFB)
            pair_statistics(p)
            normalise_out(2 * p)
            normalise_out(2 * p + 1)
            if p:
                residual_out(2 * p - 2)
                residual_out(2 * p - 1)
        residual_out(NB - 2)
        residual_out(NB - 1)
        sp.wait(added["out"])

        block = ctx.enter_context(nc.Block())

        @block.sync
        def _(e):
            sp.emit(e)

        @block.gpsimd
        def _(e):
            pool.emit(e)

        @block.scalar
        def _(e):
            actq.emit(e)

        @block.vector
        def _(e):
            dve.emit(e)

        @block.tensor
        def _(e):
            pe.emit(e)


def shape_constants(T, d, NT, cap):
    import numpy as np
    half = T // 2
    pos = np.arange(T, dtype=np.float32)[:, None]
    i = np.arange(0, d, 2, dtype=np.float32)
    inv_freq = np.exp(-(np.log(np.float32(10000.0)) * i / np.float32(d))).astype(np.float32)
    ang = (pos * inv_freq).astype(np.float32)
    pe = np.zeros((T, d), np.float32)
    pe[:, 0::2], pe[:, 1::2] = np.sin(ang), np.cos(ang)
    ident = np.eye(d, dtype=np.float32)
    pe_t = (pe.T * np.float32(float(d) ** -0.25)).astype(np.float32)
    keys = np.broadcast_to(-np.arange(half, dtype=np.float32), (d, half))
    slots = np.broadcast_to(np.arange(cap, dtype=np.float32), (d, cap))
    causal = np.where(np.arange(d)[None, :] > np.arange(d)[:, None], MASKED, 0.0).astype(np.float32)
    return np.ascontiguousarray(np.concatenate([ident, pe_t, keys, slots, causal], axis=1))


def kernel(**inputs):
    import numpy as np
    import concourse.bacc as bacc
    from concourse.bass_utils import run_bass_kernel_spmd

    a = {k: np.asarray(v) for k, v in inputs.items()}
    x = a["L0_attn_x"]
    B, T, E = x.shape
    nq = a["L0_attn_wq"].shape[1] // P
    arrays = {
        "x": x,
        "wq": a["L0_attn_wq"],
        "bqT": a["L0_attn_bq"].reshape(nq, P).T,
        "wkv": a["L0_attn_wkv"],
        "bkvT": a["L0_attn_bkv"].reshape(-1, P).T,
        "wo": a["L0_attn_wo"],
        "gwT": a["L0_ffn_gate_w"].T,
        "w_gate": a["L0_ffn_w_gate"],
        "w_up": a["L0_ffn_w_up"],
        "w_down": a["L0_ffn_w_down"],
        "sgT": a["L0_ffn_sh_gate"].T,
        "suT": a["L0_ffn_sh_up"].T,
        "sdT": a["L0_ffn_sh_down"].T,
        "consts": shape_constants(T, P, B * T, CAP),
    }
    arrays = {k: np.ascontiguousarray(v) for k, v in arrays.items()}
    nc = bacc.Bacc("TRN2", target_bir_lowering=False, num_devices=1)
    args = [nc.dram_tensor(f"in_{k}", v.shape, mybir.dt.from_np(v.dtype), kind="ExternalInput").ap()
            for k, v in arrays.items()]
    out = nc.dram_tensor("out_0", x.shape, F32, kind="ExternalOutput").ap()
    build(nc, *args, out)
    r = run_bass_kernel_spmd(nc, [{f"in_{k}": v for k, v in arrays.items()}], core_ids=[0])
    return r.results[0]["out_0"]
```

```python
from contextlib import ExitStack

import concourse.bass as bass
from concourse import mybir

F32 = mybir.dt.float32
F32R = mybir.dt.float32r
BF16 = mybir.dt.bfloat16
I32 = mybir.dt.int32
U32 = mybir.dt.uint32
ALU = mybir.AluOpType
ACT = mybir.ActivationFunctionType
AX = mybir.AxisListType.X

P = 128
TOP_K = 6
CAP = 64
EPS = 1e-5
MAGIC = 0x5F3759DF
BIG = 3.0e38
MASKED = -1.0e30


class Queue:

    def __init__(self, sem):
        self.sem, self.count, self.steps, self.seen = sem, 0, [], {}

    def wait(self, *tokens):
        for token in tokens:
            if token is None:
                continue
            if isinstance(token, list):
                self.wait(*token)
                continue
            sem, value = token
            if self.seen.get(sem.name, 0) < value:
                self.seen[sem.name] = value
                self.steps.append(lambda e, s=sem, v=value: e.wait_ge(s, v))

    def run(self, make):
        self.steps.append(make)

    def done(self, make):
        self.count += 1
        self.steps.append(lambda e, s=self.sem: make(e).then_inc(s, 1))
        return self.sem, self.count

    def emit(self, engine):
        for step in self.steps:
            step(engine)


class Slot:

    def __init__(self, sem):
        self.sem, self.count = sem, 0

    def start(self, queue, out, in_):
        self.count += 16
        queue.steps.append(lambda e, s=self.sem: e.dma_start(out, in_).then_inc(s, 16))
        return self.sem, self.count


def build(nc, x, wq, bqT, wkv, bkvT, wo, gwT, w_gate, w_up, w_down, sgT, suT, sdT, consts, out):
    NB, T, E = x.shape
    NQ = wq.shape[1] // P
    NG = wkv.shape[1] // (2 * P)
    QPG = NQ // NG
    TT = T // P
    EC = E // P
    NE, _, F = w_gate.shape
    FS = sgT.shape[1]
    NT = NB * T
    FCH = [(f, min(P, FS - f)) for f in range(0, FS, P)]
    HT = T // 2
    F2 = F // 2
    ROW = E + NE
    TRASH = CAP
    SUMROWS = NT + TRASH
    S4 = float(P) ** -0.25
    assert T == 512 and E == 256 and F % 2 == 0 and NE == 64
    assert TOP_K + 2 == 8

    table = nc.dram_tensor("token_table", [NT + 1, ROW], F32, kind="Internal").ap()
    x2_dram = nc.dram_tensor("x2_rows", [NT, E], F32, kind="Internal").ap()
    sums = nc.dram_tensor("ffn_sums", [2 * SUMROWS, E], F32, kind="Internal").ap()

    with ExitStack() as ctx:
        def sem(name):
            return ctx.enter_context(nc.semaphore(name))

        at = [0]
        base = nc.sbuf_usable_end - nc.sbuf_bytes_remaining
        at[0] = (base + 31) // 32 * 32

        def place(name, shape, dt):
            size = 4 if dt in (F32, F32R, I32, U32) else 2
            for n in shape[1:]:
                size *= n
            t = nc.alloc_sbuf_tensor_at(name, shape, dt, offset=at[0])
            at[0] += (size + 31) // 32 * 32
            return t

        weights_at = at[0]
        wq_h, wq_l = (place(f"wq_{s}", [P, EC, NQ * P], F32R) for s in "hl")
        wkv_h, wkv_l = (place(f"wkv_{s}", [P, EC, 2 * NG * P], F32R) for s in "hl")
        wkv_end = at[0]
        wo_h, wo_l = (place(f"wo_{s}", [P, NQ, E], F32R) for s in "hl")
        weights_end = at[0]
        sg_h, sg_l = (place(f"sg_{s}", [P, EC, FS], F32R) for s in "hl")
        su_h, su_l = (place(f"su_{s}", [P, EC, FS], F32R) for s in "hl")
        sd_h, sd_l = (place(f"sd_{s}", [P, len(FCH), E], F32R) for s in "hl")
        gw = place("gw", [P, EC, 2, NE], F32R)
        ident = place("ident", [P, P], F32)
        pe_t = place("pe_t", [P, T], F32)
        key_row = place("key_row", [P, HT], F32)
        slot_row = place("slot_row", [P, CAP], F32)
        ident_b = place("ident_b", [P, P], BF16)
        causal_b = place("causal_b", [P, P], BF16)
        bq_s = place("bq_s", [P, NQ], F32)
        bkv_s = place("bkv_s", [P, 2 * NG], F32)
        bk4 = place("bk4", [P, 2 * NG], F32)
        work_at = at[0]
        xn_h, xn_l = (place(f"xn_{s}", [P, EC, T], F32R) for s in "hl")
        k_h, k_l = (place(f"k_{s}", [P, NG, T], F32R) for s in "hl")
        v_h, v_l = (place(f"v_{s}", [P, TT, NG * P], F32R) for s in "hl")
        heads_at = at[0]
        q_sum = place("q_sum", [P, T], F32)
        q_h, q_l = (place(f"q_{s}", [P, 2, T], F32R) for s in "hl")
        tri = [P * (i * (i + 1) // 2) for i in range(TT + 1)]
        inv = [P * (TT * j - j * (j - 1) // 2) for j in range(TT + 1)]
        prob = place("prob", [P, 2, tri[TT]], F32)
        pt_h, pt_l = (place(f"pt_{s}", [P, tri[TT]], F32R) for s in "hl")
        negmax = place("negmax", [P, 2, TT], F32)
        rsum = place("rsum", [P, 2, TT], F32)
        rinv = place("rinv", [P, 2, TT], F32)
        heads_end = at[0]
        xio = place("xio", [P, TT, E], F32)
        stage_at = at[0]
        o_h, o_l = (place(f"o_{s}", [P, T], F32R) for s in "hl")
        ytr = place("ytr", [P, EC, T], F32)
        rows = place("rows", [P, TT, ROW], F32)
        x2_h, x2_l = (place(f"x2_{s}", [P, EC, HT], F32R) for s in "hl")
        sig = place("sig", [P, HT], F32)
        act = place("act", [P, HT], F32)
        a_h, a_l = (place(f"a_{s}", [P, len(FCH), HT], F32R) for s in "hl")
        stage_end = at[0]
        logit = place("logit", [P, 2, NE + 2], F32)
        top8 = place("top8", [P, 2, 8], F32)
        left = place("left", [P, 2, NE + 2], F32)
        mask = place("mask", [P, TT, NE], F32)
        rmax = place("rmax", [P, TT], F32)
        psum_ = place("router_sum", [P, TT], F32)
        pinv = place("router_inv", [P, TT], F32)
        keys = place("keys", [P, CAP + T], F32)
        first = place("first", [P, CAP], F32)
        stat = place("stat", [P, TT, 6], F32)
        mv = place("mv", [P, TT, 2], F32)
        nw = place("nw", [P, 4, TT], F32)
        zero_f = place("zero_f", [P, ROW], F32)
        end_at = at[0]
        assert end_at <= nc.sbuf_usable_end, (end_at, nc.sbuf_usable_end)
        at[0] = stage_at
        STG = 2048
        stage = [place(f"stage{i}", [P, STG], F32) for i in range(3)]
        assert at[0] <= stage_end
        at[0] = stage_end
        causal_f = place("causal_f", [P, P], F32)
        assert at[0] <= stage_end + 4 * 2 * (NE + 2) + 4 * 16 + 4 * 2 * (NE + 2)
        at[0] = weights_at
        NW = 16
        w_gu, w_dn = [], []
        w_where = []
        for s in range(NW):
            w_gu.append(place(f"w_gu{s}", [P, 2, 2 * F], F32))
            w_dn.append(place(f"w_dn{s}", [P, 2, E], F32))
            w_where.append(at[0])
        assert at[0] <= weights_end
        at[0] = heads_at
        NX, ND = 5, 3
        xg = [place(f"xg{i}", [P, ROW], F32) for i in range(NX)]
        xt = [place(f"xt{i}", [P, EC, P], F32) for i in range(2)]
        ex = [place(f"ex{i}", [P, F], F32) for i in range(2)]
        half_w = [place(f"half_w{i}", [P, 1], F32) for i in range(2)]
        ag = [place(f"ag{i}", [P, F], F32) for i in range(2)]
        atr = [place(f"atr{i}", [P, 2, P], F32) for i in range(2)]
        dsum = [place(f"dsum{i}", [P, E], F32) for i in range(ND)]
        tok2 = place("tok2", [P, 2 * CAP], F32)
        sct2 = place("sct2", [P, 2 * CAP], F32)
        empty = place("empty", [P, CAP], F32)
        idx_g = place("idx_g", [P, NE // 2], I32)
        idx_s = place("idx_s", [P, NE // 2], I32)
        after_experts = at[0]
        x2b_h, x2b_l = (place(f"x2b_{s}", [P, EC, HT], F32R) for s in "hl")
        ab_h, ab_l = (place(f"ab_{s}", [P, len(FCH), HT], F32R) for s in "hl")
        sig_b = place("sig_b", [P, HT], F32)
        act_b = place("act_b", [P, HT], F32)
        assert at[0] <= heads_end, (at[0], heads_end)
        at[0] = after_experts
        NFB = 4
        fa = [place(f"fa{b}", [P, TT, E], F32) for b in range(NB)]
        fstat = [place(f"fstat{i}", [P, 2 * TT, 6], F32) for i in range(2)]
        fmv = [place(f"fmv{i}", [P, 2 * TT, 2], F32) for i in range(2)]
        fnw = [place(f"fnw{i}", [P, 4, 2 * TT], F32) for i in range(2)]
        fb = [place(f"fb{i}", [P, TT, E], F32) for i in range(2)]
        assert at[0] <= end_at, (at[0], end_at)
        at[0] = work_at
        fb += [place(f"fb{i}", [P, TT, E], F32) for i in range(2, NFB)]
        fx = [place(f"fx{b}", [P, TT, E], F32) for b in range(NB)]

        bank = {n: ctx.enter_context(nc.psum_tensor(f"bank_{n}", [P, 512], F32))
                for n in ("s0", "s1", "t0", "t1", "o", "y0", "y1", "f")}
        free = {n: None for n in bank}

        pe, dve, actq, pool, sp = (Queue(sem(f"{n}_done")) for n in ("pe", "dve", "act", "pool", "sp"))

        def mm(o, l, r, start=False, stop=False, last=False):
            def make(e):
                return e.matmul(o, l, r, start=start, stop=stop, skip_group_check=True)
            return pe.done(make) if last else pe.run(make)

        def mm3(o, l, r, start, last=False):
            mm(o, l[0], r[0], start=start)
            mm(o, l[0], r[1])
            return mm(o, l[1], r[0], stop=True, last=last)

        def tr(o, i, idn, last=False):
            def make(e):
                return e.transpose(o, i, idn)
            return pe.done(make) if last else pe.run(make)

        def f(ap):
            return ap.bitcast(F32)

        s_const, s_zero = Slot(sem("dma_const")), Slot(sem("dma_zero"))
        s_stage = [Slot(sem(f"dma_stage{i}")) for i in range(3)]
        s_x = Slot(sem("dma_x"))
        x_rows = x.rearrange("b (i p) e -> b p i e", p=P)

        def load_x(b, *before):
            sp.wait(*before)
            return s_x.start(sp, xio[:], x_rows[b])

        first_x = load_x(0)
        C = consts
        c0 = 0
        for t, n in ((ident, P), (pe_t, T), (key_row, HT), (slot_row, CAP), (causal_f, P)):
            const_in = s_const.start(sp, t[:, 0:n], C[:, c0:c0 + n])
            c0 += n
        s_const.start(sp, bq_s[:], bqT)
        const_in = s_const.start(sp, bkv_s[:], bkvT)

        pieces = []
        for c in range(EC):
            pieces.append(([(wkv[c * P:(c + 1) * P, :], 0, 2 * NG * P)], P, [
                (0, 2 * NG * P, [t[:, c, :] for t in (wkv_h, wkv_l)], "kv")]))
        for k in range(2):
            n = NQ * P // 2
            cols = slice(k * n, (k + 1) * n)
            pieces.append(([(wq[:, cols].rearrange("(c p) n -> p c n", p=P), 0, EC * n)], P, [
                (c * n, n, [t[:, c, cols] for t in (wq_h, wq_l)], S4) for c in range(EC)]))
        for c in range(2):
            n = NQ // 2
            pieces.append(([(wo[c * n * P:(c + 1) * n * P, :].rearrange("(h p) e -> p h e", p=P), 0, n * E)], P, [
                (0, n * E, [t[:, c * n:(c + 1) * n, :].rearrange("p h e -> p (h e)") for t in (wo_h, wo_l)], 1.0)]))
        pieces.append(([(sgT.rearrange("(c p) f -> p c f", p=P), 0, EC * FS),
                        (suT.rearrange("(c p) f -> p c f", p=P), EC * FS, EC * FS),
                        (gwT.rearrange("(c p) f -> p c f", p=P), 2 * EC * FS, EC * NE)], P, [
            (0, EC * FS, [t[:, :, :].rearrange("p c f -> p (c f)") for t in (sg_h, sg_l)], 1.0),
            (EC * FS, EC * FS, [t[:, :, :].rearrange("p c f -> p (c f)") for t in (su_h, su_l)], 1.0),
            *((2 * EC * FS + c * NE, NE, [gw[:, c, s, :] for s in range(2)], 1.0) for c in range(EC))]))
        whole = [q for q in FCH if q[1] == P]
        pieces.append(([(sdT[0:P * len(whole), :].rearrange("(c p) e -> p c e", p=P), 0, len(whole) * E)], P, [
            (0, len(whole) * E, [t[:, 0:len(whole), :].rearrange("p c e -> p (c e)") for t in (sd_h, sd_l)], 1.0)]))
        if len(whole) < len(FCH):
            r0, rn = FCH[-1]
            pieces.append(([(sdT[r0:r0 + rn, :], 0, E)], rn, [
                (0, E, [t[0:rn, len(whole), :] for t in (sd_h, sd_l)], 1.0)]))

        stage_free = [None] * 3
        split = []

        def load_piece(n):
            sources, rowsn, _ = pieces[n]
            sp.wait(stage_free[n % 3])
            for src, a, w in sources:
                dst = stage[n % 3][0:rowsn, a:a + w]
                if len(src.shape) == 3:
                    dst = dst.rearrange("p (c f) -> p c f", c=src.shape[1])
                tok = s_stage[n % 3].start(sp, dst, src)
            return tok

        def split_piece(n, tok, width=STG):
            _, rowsn, parts = pieces[n]
            low = None
            for a, w, (hi, lo), scale in parts:
                src = stage[n % 3][0:rowsn, a:a + w]
                chunks = [slice(c, min(c + width, w)) for c in range(0, w, width)]
                todo = [(src[:, c], hi[:, c], lo[:, c], scale) for c in chunks]
                if scale == "kv":
                    v = [t.rearrange("p (g two d) -> p g two d", two=2, d=P) for t in (src, hi, lo)]
                    todo = [(*[t[:, :, k, :] for t in v], (S4, 1.0)[k]) for k in range(2)]
                for s_, h_, l_, m_ in todo:
                    yield
                    actq.wait(tok)
                    t1 = actq.done(lambda e, s_=s_, h_=h_, m_=m_: e.activation(h_, s_, ACT.Copy, scale=m_))
                    if low:
                        low()

                    def low(t1=t1, s_=s_, h_=h_, l_=l_, m_=m_):
                        dve.wait(tok, t1)
                        return dve.done(lambda e: e.scalar_tensor_tensor(
                            out=l_, in0=s_, scalar=m_, in1=f(h_), op0=ALU.mult, op1=ALU.subtract))
            yield
            stage_free[n % 3] = low()
            split.append(stage_free[n % 3])

        toks = [load_piece(n) for n in range(3)]
        zeroed = pool.done(lambda e: e.memset(zero_f[:], 0.0))
        dve.wait(const_in)
        dve.run(lambda e: e.tensor_copy(ident_b[:], ident[:]))
        dve.wait(dve.done(lambda e: e.tensor_copy(causal_b[:], causal_f[:])))
        dve.run(lambda e: e.memset(logit[:, :, NE:NE + 2], BIG))
        dve.run(lambda e: e.memset(keys[0:NE, 0:CAP], 0.0))
        dve.run(lambda e: e.tensor_scalar(bk4[:], bkv_s[:], S4, None, ALU.mult))
        bq_ready = dve.done(lambda e: e.tensor_scalar(bq_s[:], bq_s[:], S4, None, ALU.mult))
        dve.wait(bq_ready)

        def statistics(sources, statt, mvt, nwt, n0):
            n = len(sources)
            v, y, a = nwt[:, 0, n0:n0 + n], nwt[:, 1, n0:n0 + n], nwt[:, 2, n0:n0 + n]

            def newton():
                pool.wait(pool.done(lambda e: e.tensor_tensor(a, y, y, ALU.mult)))
                pool.wait(pool.done(lambda e: e.tensor_tensor(a, a, v, ALU.mult)))
                pool.wait(pool.done(lambda e: e.tensor_scalar(a, a, -0.5, 1.5, ALU.mult, ALU.add)))
                t = pool.done(lambda e: e.tensor_tensor(y, a, y, ALU.mult))
                pool.wait(t)
                return t

            for i, s_ in enumerate(sources):
                t = dve.done(lambda e, s_=s_, i=i: e.bn_stats(statt[:, n0 + i, :], s_))
            dve.wait(t)
            for i in range(n):
                t = dve.done(lambda e, i=i: e.bn_aggr(mvt[:, n0 + i, :], statt[:, n0 + i, :]))
            var = mvt[:, n0:n0 + n, 1:2].rearrange("p i o -> p (i o)")
            dve.wait(t)
            dve.wait(dve.done(lambda e: e.tensor_scalar(v, var, EPS, None, ALU.add)))
            dve.wait(dve.done(lambda e: e.tensor_scalar(a.bitcast(I32), v.bitcast(I32), 1, None,
                                                        ALU.logical_shift_right)))
            pool.wait(dve.done(lambda e: e.tensor_scalar(y.bitcast(I32), a.bitcast(I32), -1.0, float(MAGIC),
                                                         ALU.mult, ALU.add)))
            newton()
            yield "C"
            newton()
            yield "C"
            return newton()

        def statistics_now(*args):
            parts = statistics(*args)
            while True:
                try:
                    next(parts)
                except StopIteration as end:
                    return end.value

        def normed(o, s_, mvt, nwt, i):
            return dve.done(lambda e: e.tensor_scalar(o, s_, mvt[:, i, 0:1], nwt[:, 1, i:i + 1],
                                                      ALU.subtract, ALU.mult))

        ready = {}
        last_read = {}
        x_in = {}
        made_for = {}

        def norm_x(b):
            yield "C"
            dve.wait(x_in[b])
            ready["xstat"] = yield from statistics([xio[:, i, :] for i in range(TT)], stat, mv, nw, 0)
            yield "C"
            dve.wait(ready["xstat"])
            for i in range(TT):
                ready["xnorm"] = normed(xio[:, i, :], xio[:, i, :], mv, nw, i)

        def turn_x(c, bk="f"):
            yield "P"
            pe.wait(ready["xnorm"], free[bk], const_in)
            for i in range(TT):
                t = tr(bank[bk][:, i * P:(i + 1) * P], xio[:, i, c * P:(c + 1) * P], ident[:], last=i == TT - 1)
            last_read["xio"] = t
            yield "C"
            actq.wait(t, last_read.get("xn"))
            t = actq.done(lambda e: e.activation(xn_h[:, c, :], bank[bk][:], ACT.Copy))
            dve.wait(t)
            t = dve.done(lambda e: e.tensor_tensor(xn_l[:, c, :], bank[bk][:], f(xn_h[:, c, :]), ALU.subtract))
            free[bk] = ready["xn"] = t
            if c == EC - 1:
                made_for["xn"] = made_for.get("xn", -1) + 1

        def project(bk, hi, lo, col):
            pe.wait(free[bk], ready["xn"])
            for c in range(EC):
                t = mm3(bank[bk][:], [w[:, c, col:col + P] for w in (hi, lo)],
                        [a[:, c, :] for a in (xn_h, xn_l)], start=c == 0, last=c == EC - 1)
            last_read["xn"] = t
            return t

        def with_position(bk, t, bias, h_, l_, before):
            dve.wait(t, last_read.get("q_sum"))
            t = dve.done(lambda e: e.scalar_tensor_tensor(out=q_sum[:], in0=bank[bk][:], scalar=bias,
                                                          in1=pe_t[:], op0=ALU.add, op1=ALU.add))
            free[bk] = t
            actq.wait(t, before)
            t = actq.done(lambda e: e.activation(h_, q_sum[:], ACT.Copy))
            pool.wait(t)
            made = []
            for part_ in (slice(T - P, T), slice(0, T - P)):
                made.append(pool.done(lambda e, q=part_: e.tensor_tensor(l_[:, q], q_sum[:, q], f(h_)[:, q],
                                                                         ALU.subtract)))
            last_read["q_sum"] = made[1]
            return made

        def make_k(g, bk="f"):
            yield "P"
            pe.wait(split[1])
            t = project(bk, wkv_h, wkv_l, 2 * g * P)
            yield "C"
            made_for["k", g] = made_for.get(("k", g), -1) + 1
            ready["k", g] = with_position(bk, t, bk4[:, 2 * g:2 * g + 1], k_h[:, g, :], k_l[:, g, :],
                                          last_read.get(("k", g)))

        def make_v(half, s2, bk="f"):
            yield "P"
            pe.wait(free[bk], ready["xn"], split[1])
            ng = NG // 2
            g0 = half * ng
            views = [w[:, :, :].rearrange("p c (g two d) -> p c g two d", two=2, d=P)[:, :, g0:g0 + ng, 1, :]
                     for w in (wkv_h, wkv_l)]
            for k in range(2):
                s = 2 * s2 + k
                o = bank[bk][:, k * ng * P:(k + 1) * ng * P]
                for c in range(EC):
                    t = mm3(o, [a[:, c, s * P:(s + 1) * P] for a in (xn_h, xn_l)],
                            [w[:, c] for w in views], start=c == 0, last=c == EC - 1)
            last_read["xn"] = t
            yield "C"
            src = bank[bk][:].rearrange("p (s n) -> p s n", s=2)
            h_, l_ = (v[:, 2 * s2:2 * s2 + 2, g0 * P:(g0 + ng) * P] for v in (v_h, v_l))
            actq.wait(t, last_read.get(("v", half)))
            t = actq.done(lambda e: e.activation(h_, src, ACT.Copy))
            dve.wait(t)
            t = dve.done(lambda e: e.tensor_tensor(l_, src, f(h_), ALU.subtract))
            free[bk] = ready["v", half] = t
            if s2 == TT // 2 - 1:
                made_for["v", half] = made_for.get(("v", half), -1) + 1

        def make_q(n, bk="f"):
            h = n % NQ
            yield "P"
            pe.wait(split[2 + (h >= NQ // 2)])
            assert made_for["xn"] == n // NQ
            t = project(bk, wq_h, wq_l, h * P)
            yield "C"
            ready["q", n] = with_position(bk, t, bq_s[:, h:h + 1], q_h[:, n % 2, :], q_l[:, n % 2, :],
                                          last_read.get(("q", n - 2)))

        def at_once(gen):
            for _ in gen:
                pass

        def scores(n, i):
            h, r = n % NQ, n % 2
            g, w, bk = h // QPG, (i + 1) * P, f"s{i % 2}"
            assert made_for["k", g] == n // NQ
            pe.wait(free[bk], ready["q", n][i < TT - 1], ready["k", g])
            mm(bank[bk][:, i * P:w], ident_b[:], causal_b[:], start=True)
            t = mm3(bank[bk][:, 0:w], [q[:, r, i * P:(i + 1) * P] for q in (q_h, q_l)],
                    [k[:, g, 0:w] for k in (k_h, k_l)], start=False, last=True)
            last_read["q", n] = last_read["k", g] = t
            dve.wait(t, ready.get(("exp", n - 2, i)))
            ready["max", n, i] = dve.done(lambda e: e.reduce_max(negmax[:, r, i:i + 1], bank[bk][:, 0:w], AX,
                                                                 negate=True))

        def exponentials(n, i):
            r, w, bk = n % 2, (i + 1) * P, f"s{i % 2}"
            actq.wait(ready["max", n, i], ready.get(("turned", n - 2)), ready.get(("rinv", n - 2, i)))
            t = actq.done(lambda e: e.activation(prob[:, r, tri[i]:tri[i + 1]], bank[bk][:, 0:w], ACT.Exp,
                                                 bias=negmax[:, r, i:i + 1], accum_out=rsum[:, r, i:i + 1]))
            free[bk] = ready["exp", n, i] = t

        def normalise(n, i):
            r = n % 2
            dve.wait(ready["exp", n, i], ready.get(("normal", n - 2, i)))
            t = dve.done(lambda e: e.reciprocal(rinv[:, r, i:i + 1], rsum[:, r, i:i + 1]))
            ready["rinv", n, i] = t
            pool.wait(t)
            p_ = prob[:, r, tri[i]:tri[i + 1]]
            w = (i + 1) * P
            ready["normal", n, i] = pool.done(lambda e: e.tensor_tensor(
                p_, p_, rinv[:, r, i:i + 1].to_broadcast([P, w]), ALU.mult))

        def turn(n, j):
            r, bk = n % 2, f"t{j % 2}"
            pe.wait(free[bk], [ready["normal", n, i] for i in range(j, TT)])
            for i in range(j, TT):
                t = tr(bank[bk][:, (i - j) * P:(i - j + 1) * P],
                       prob[:, r, tri[i] + j * P:tri[i] + (j + 1) * P], ident[:], last=i == TT - 1)
            ready["turn", n, j] = t
            if j == 0:
                ready["turned", n] = t

        def turned_high(n, j):
            bk, w, h_ = f"t{j % 2}", (TT - j) * P, pt_h[:, inv[j]:inv[j + 1]]
            actq.wait(ready["turn", n, j], last_read.get(("pt", j)))
            ready["pth", n, j] = actq.done(lambda e: e.activation(h_, bank[bk][:, 0:w], ACT.Copy))

        def turned_low(n, j):
            bk, w = f"t{j % 2}", (TT - j) * P
            h_, l_ = (q[:, inv[j]:inv[j + 1]] for q in (pt_h, pt_l))
            dve.wait(ready["pth", n, j])
            t = dve.done(lambda e: e.tensor_tensor(l_, bank[bk][:, 0:w], f(h_), ALU.subtract))
            free[bk] = ready["pt", n, j] = t

        def values(n, j):
            g = n % NQ // QPG
            assert made_for["v", g // (NG // 2)] == n // NQ
            pe.wait(ready["pt", n, j], ready["v", g // (NG // 2)])
            if j == TT - 1:
                pe.wait(free["o"])
            t = mm3(bank["o"][:, j * P:T], [v[:, j, g * P:(g + 1) * P] for v in (v_h, v_l)],
                    [q[:, inv[j]:inv[j + 1]] for q in (pt_h, pt_l)], start=j == TT - 1, last=True)
            last_read["pt", j] = last_read["v", g // (NG // 2)] = t
            ready["o_bank"] = t

        def output_high(n):
            g = n % NQ // QPG
            bias = bkv_s[:, 2 * g + 1:2 * g + 2]
            actq.wait(ready["o_bank"], last_read.get("o"))
            ready["oh"] = actq.done(lambda e: e.activation(o_h[:], bank["o"][:], ACT.Identity, bias=bias))

        def output_low(n):
            g = n % NQ // QPG
            bias = bkv_s[:, 2 * g + 1:2 * g + 2]
            dve.wait(ready["oh"])
            free["o"] = ready["o"] = dve.done(lambda e: e.scalar_tensor_tensor(
                out=o_l[:], in0=bank["o"][:], scalar=bias, in1=f(o_h[:]), op0=ALU.add, op1=ALU.subtract))

        def project_out(n):
            h = n % NQ
            pe.wait(ready["o"], split[5])
            if h == 0:
                pe.wait(free["y0"], free["y1"])
            for c in range(EC):
                t = mm3(bank[f"y{c}"][:], [w[:, h, c * P:(c + 1) * P] for w in (wo_h, wo_l)],
                        [o_h[:], o_l[:]], start=h == 0, last=c == EC - 1)
            last_read["o"] = t
            if h == NQ - 1:
                actq.wait(t, last_read.get("ytr"))
                dve.wait(t, last_read.get("ytr"))
                free["y0"] = actq.done(lambda e: e.activation(ytr[:, 0, :], bank["y0"][:], ACT.Copy))
                free["y1"] = dve.done(lambda e: e.tensor_copy(ytr[:, 1, :], bank["y1"][:]))
                ready["ytr"] = [free["y0"], free["y1"]]

        s_x2, s_rows, s_ffn = Slot(sem("dma_x2")), Slot(sem("dma_rows")), [Slot(sem(f"dma_ffn{k}")) for k in range(2)]
        stored = {}
        x2_rows = x2_dram.rearrange("(b i p) e -> b p i e", p=P, i=TT)
        table_rows = table[0:NT, :].rearrange("(b i p) e -> b p i e", p=P, i=TT)
        sum_rows = [sums[a * SUMROWS:a * SUMROWS + NT, :].rearrange("(b i p) e -> b p i e", p=P, i=TT)
                    for a in range(2)]
        pick_of = {}

        def pick(b):
            span = keys[0:NE, :]
            for r in range(CAP // 8):
                yield "C"
                o_ = first[0:NE, 8 * r:8 * r + 8]
                dve.wait(ready["keys"])
                dve.wait(dve.done(lambda e, o_=o_: e.max(o_, span)))
                if r < CAP // 8 - 1:
                    dve.wait(dve.done(lambda e, o_=o_: e.match_replace(span, o_, span, 0.0)))
            dve.wait(dve.done(lambda e: e.tensor_copy(keys[0:NE, 0:CAP], first[0:NE, :])))

        def token_norms(b, banks):
            yield "C"
            x_again = load_x(b, last_read["xio"])
            for k in range(2):
                yield "P"
                bk = banks[k]
                bf = bank[bk]
                pe.wait(free[bk], ready["ytr"])
                for i in range(2):
                    for c in range(EC):
                        t = tr(bf[:, i * E + c * P:i * E + (c + 1) * P],
                               ytr[:, c, (2 * k + i) * P:(2 * k + i + 1) * P], ident[:],
                               last=(i, c) == (1, EC - 1))
                last_read["ytr"] = t
                yield "C"
                actq.wait(t, stored.get("rows"))
                t = free[bk] = actq.done(lambda e, k=k, bf=bf: e.activation(
                    rows[:, 2 * k:2 * k + 2, 0:E], bf[:].rearrange("p (i e) -> p i e", i=2), ACT.Copy))
            yield "C"
            dve.wait(t)
            t = yield from statistics([rows[:, i, 0:E] for i in range(TT)], stat, mv, nw, 0)
            yield "C"
            dve.wait(t)
            for i in range(TT):
                t = normed(rows[:, i, 0:E], rows[:, i, 0:E], mv, nw, i)
            pool.wait(t, x_again)
            t = pool.done(lambda e: e.tensor_tensor(xio[:], xio[:], rows[:, :, 0:E], ALU.add))
            yield "C"
            yield "C"
            dve.wait(t)
            sp.wait(t)
            stored["x2"] = s_x2.start(sp, x2_rows[b], xio[:])
            t2 = yield from statistics([xio[:, i, :] for i in range(TT)], stat, mv, nw, 0)
            yield "C"
            dve.wait(t2)
            for i in range(TT):
                t = normed(rows[:, i, 0:E], xio[:, i, :], mv, nw, i)
            ready["ln2"] = t
            last_read["xio"] = [stored["x2"], t]

        lanes = [(x2_h, x2_l, a_h, a_l, sig, act), (x2b_h, x2b_l, ab_h, ab_l, sig_b, act_b)]

        def route(b, k, bk, lane):
            bf = bank[bk]
            x2h, x2l = lanes[lane][0:2]
            k2 = slice(2 * k, 2 * k + 2)
            yield "P"
            pe.wait(ready["ln2"], free[bk])
            for c in range(EC):
                for i in range(2):
                    t = tr(bf[:, c * HT + i * P:c * HT + (i + 1) * P],
                           rows[:, 2 * k + i, c * P:(c + 1) * P], ident[:], last=(c, i) == (EC - 1, 1))
            yield "C"
            src = bf[:].rearrange("p (c t) -> p c t", c=EC)
            actq.wait(t, last_read.get(("x2", lane)))
            t = actq.done(lambda e, src=src: e.activation(x2h[:], src, ACT.Copy))
            dve.wait(t)
            t = dve.done(lambda e, src=src: e.tensor_tensor(x2l[:], src, f(x2h[:]), ALU.subtract))
            free[bk] = ready["x2", lane] = t
            yield "P"
            pe.wait(ready["x2", lane], free[bk], split[6])
            for i in range(2):
                o_ = bf[:, 2 * i * NE:2 * (i + 1) * NE]
                for c in range(EC):
                    xh, xl = (a[:, c, i * P:(i + 1) * P] for a in (x2h, x2l))
                    mm(o_, xh, gw[:, c, :, :].rearrange("p s n -> p (s n)"), start=c == 0)
                    t = mm(o_[:, 0:NE], xl, gw[:, c, 0, :], stop=c == EC - 1, last=c == EC - 1)
            yield "C"
            dve.wait(t, ready.get("router_exp"))
            halves = bf[:, 0:4 * NE].rearrange("p (i s n) -> p i s n", i=2, s=2)
            dve.wait((dve.sem, dve.count))
            low_done = dve.done(lambda e: e.tensor_copy(left[:, :, 0:NE], halves[:, :, 1, :]))
            dve.wait(low_done)
            t = dve.done(lambda e: e.tensor_tensor(logit[:, :, 0:NE], halves[:, :, 0, :], left[:, :, 0:NE], ALU.add))
            free[bk] = t
            dve.wait(t)
            for i in range(2):
                t = dve.done(lambda e, i=i: e.max(top8[:, i, :], logit[:, i, :]))
            dve.wait(t)
            t2 = dve.done(lambda e: e.tensor_scalar(rmax[:, k2], top8[:, :, 2:3].rearrange("p i o -> p (i o)"),
                                                    -1.0, None, ALU.mult))
            for i in range(2):
                t = dve.done(lambda e, i=i: e.match_replace(left[:, i, :], top8[:, i, :], logit[:, i, :], -BIG))
            dve.wait(t, last_read.get(("mask", k)))
            ready["mask", k] = dve.done(lambda e: e.tensor_scalar(mask[:, k2, :], left[:, :, 0:NE], -BIG, None,
                                                               ALU.is_equal))
            actq.wait(t2)
            for i in range(2):
                o_ = rows[:, 2 * k + i, E:ROW]
                t = actq.done(lambda e, i=i, o_=o_: e.activation(o_, logit[:, i, 0:NE], ACT.Exp,
                                                                 bias=rmax[:, 2 * k + i:2 * k + i + 1],
                                                                 accum_out=psum_[:, 2 * k + i:2 * k + i + 1]))
            ready["router_exp"] = t
            yield "C"
            yield "P"
            pe.wait(ready["mask", k], free[bk])
            for i in range(2):
                t = tr(bf[0:NE, i * P:(i + 1) * P], mask[:, 2 * k + i, :], ident[:], last=i == 1)
            last_read["mask", k] = t
            yield "C"
            if k == 0 and b:
                at_once(pick_of.pop(b - 1, ()))
            off = float(NT - b * T - k * HT)
            o_ = keys[0:NE, CAP + k * HT:CAP + (k + 1) * HT]
            dve.wait(t)
            t = dve.done(lambda e, off=off, o_=o_: e.scalar_tensor_tensor(
                out=o_, in0=key_row[0:NE, :], scalar=off, in1=bf[0:NE, 0:HT],
                op0=ALU.add, op1=ALU.mult))
            free[bk] = ready["keys"] = t
            if k == 1:
                pick_of[b] = pick(b)
            dve.wait(ready["router_exp"])
            t = dve.done(lambda e: e.reciprocal(pinv[:, k2], psum_[:, k2]))
            dve.wait(t)
            for i in range(2):
                o_ = rows[:, 2 * k + i, E:ROW]
                inv_ = pinv[:, 2 * k + i:2 * k + i + 1]
                t = dve.done(lambda e, o_=o_, inv_=inv_: e.tensor_scalar(o_, o_, inv_, None, ALU.mult))
            if k == 1:
                sp.wait(t)
                stored["rows"] = s_rows.start(sp, table_rows[b], rows[:])

        def shared_expert(b, k, bk, lane):
            bf = bank[bk]
            x2h, x2l, ah, al, sg_, ac_ = lanes[lane]
            for n, (f0, fn) in enumerate(FCH):
                yield "P"
                pe.wait(free[bk], ready["x2", lane], split[-1])
                for u, (hi, lo) in enumerate(((sg_h, sg_l), (su_h, su_l))):
                    for c in range(EC):
                        t = mm3(bf[0:fn, u * HT:(u + 1) * HT], [w[:, c, f0:f0 + fn] for w in (hi, lo)],
                                [a[:, c, :] for a in (x2h, x2l)], start=c == 0, last=c == EC - 1)
                last_read["x2", lane] = t
                yield "C"
                gate, up = bf[0:fn, 0:HT], bf[0:fn, HT:2 * HT]
                s_, a_ = sg_[0:fn, :], ac_[0:fn, :]
                actq.wait(t, ready.get(("act", lane)))
                t = actq.done(lambda e, s_=s_, gate=gate: e.activation(s_, gate, ACT.Tanh, scale=0.5))
                dve.wait(t)
                t = dve.done(lambda e, s_=s_, gate=gate: e.scalar_tensor_tensor(
                    out=s_, in0=s_, scalar=1.0, in1=gate, op0=ALU.add, op1=ALU.mult))
                dve.wait(t, last_read.get(("act", lane)))
                t = dve.done(lambda e, s_=s_, a_=a_, up=up: e.scalar_tensor_tensor(
                    out=a_, in0=s_, scalar=0.5, in1=up, op0=ALU.mult, op1=ALU.mult))
                free[bk] = ready["act", lane] = t
                h_, l_ = (q[0:fn, n, :] for q in (ah, al))
                actq.wait(t, last_read.get(("a", lane)))
                t = actq.done(lambda e, h_=h_, a_=a_: e.activation(h_, a_, ACT.Copy))
                pool.wait(t)
                t = pool.done(lambda e, l_=l_, h_=h_, a_=a_: e.tensor_tensor(l_, a_, f(h_), ALU.subtract))
                last_read["act", lane] = t
                ready["a", lane] = t
            yield "C"
            yield "P"
            pe.wait(free[bk], ready["a", lane])
            for i in range(2):
                for n, (f0, fn) in enumerate(FCH):
                    t = mm3(bf[:, i * E:(i + 1) * E], [q[0:fn, n, i * P:(i + 1) * P] for q in (ah, al)],
                            [w[0:fn, n, :] for w in (sd_h, sd_l)], start=n == 0, last=n == len(FCH) - 1)
            last_read["a", lane] = t
            yield "C"
            o_ = ytr[:, k, :].rearrange("p (i e) -> p i e", i=2)
            actq.wait(t)
            t = actq.done(lambda e, o_=o_: e.activation(o_, bf[:].rearrange("p (i e) -> p i e", i=2), ACT.Copy))
            free[bk] = t
            sp.wait(t)
            stored["ffn", b, k] = s_ffn[k].start(sp, sum_rows[0][b, :, 2 * k:2 * k + 2, :], o_)
            last_read["ytr"] = [t, stored["ffn", b, k]]

        def token_layer(b):
            yield from token_norms(b, "ff")
            for k in range(2):
                yield from route(b, k, "f", 0)
                yield from shared_expert(b, k, "f", 0)

        x_in[0] = first_x
        norm = norm_x(0)
        for _ in range(4):
            next(norm)
        at_once(split_piece(0, toks[0]))
        at_once(split_piece(1, toks[1]))
        at_once(norm)
        at_once(turn_x(0, "s0"))
        at_once(turn_x(1, "s1"))
        at_once(split_piece(2, toks[2]))

        def split_rest():
            for n in range(3, len(pieces)):
                yield from split_piece(n, toks[n], STG // 2)
                if n + 3 < len(pieces):
                    toks.append(load_piece(n + 3))

        toks += [load_piece(n) for n in range(3, 6)]

        sp.wait(zeroed)
        zero_left = 2 * SUMROWS - NT
        per = 2048 // E * P
        n0 = NT
        while zero_left:
            m = min(per, zero_left)
            if m >= P:
                m = m // P * P
                zt = s_zero.start(sp, sums[n0:n0 + m, :].rearrange("(p r) e -> p r e", p=P),
                                  zero_f[:, 0:E].rearrange("p (o e) -> p o e", o=1).to_broadcast([P, m // P, E]))
            else:
                zt = s_zero.start(sp, sums[n0:n0 + m, :], zero_f[0:m, 0:E])
            n0 += m
            zero_left -= m
        zt = s_zero.start(sp, table[NT:NT + 1, :], zero_f[0:1, 0:ROW])
        for q in (pe, actq, pool):
            q.wait(bq_ready)
        at_once(make_k(0, "t0"))
        at_once(make_q(0))
        at_once(make_q(1))

        N = NB * NQ

        class Behind:

            def __init__(self, *gens):
                self.gens, self.tag = list(gens), None
                self.step(first=True)

            def step(self, first=False):
                while self.gens:
                    try:
                        self.tag = next(self.gens[0])
                        return
                    except StopIteration:
                        self.gens.pop(0)
                self.tag = None

        tasks = {}
        holding = [None]

        def later(kind, *gens):
            if kind in tasks:
                tasks[kind].gens += gens
            else:
                tasks[kind] = Behind(*gens)

        def part(kinds, tags):
            for kind in ([holding[0]] if holding[0] else kinds):
                task = tasks.get(kind)
                if task and task.tag in tags:
                    holding[0] = kind if task.tag == "P" else None
                    task.step()
                    if task.tag is None:
                        del tasks[kind]
                    return True
            return False

        kv_at = {0: [(make_v, 0, 0), (make_v, 0, 1)], 3: [(make_k, 1)], 5: [(make_v, 1, 0)],
                 6: [(make_v, 1, 1)], 7: [(make_k, 2)], 11: [(make_k, 3)]}

        def normalised(n, ph):
            if ph and n < N:
                normalise(n, TT - ph)
            elif not ph and 0 < n <= N:
                normalise(n - 1, 0)

        rest = split_rest()
        turns = []
        q_parts = None
        output = None
        behind = ["kv", "xnorm", "tokens"]
        ORDER = [line.split() for line in (
            "turned_high readers turned_low scores exponentials normalised",
            "readers turned_high scores turned_low exponentials normalised",
            "turned_high readers scores exponentials turned_low normalised",
            "output_high readers output_low turned_high scores turned_low exponentials normalised")]
        SPARE = 7
        for n in range(N + 3):
            b, h = n // NQ, n % NQ
            live = n < N
            if live:
                if h in kv_at:
                    later("kv", *(m(*a) for m, *a in kv_at[h]))
                if b + 1 < NB:
                    if h == NQ - 5:
                        x_in[b + 1] = load_x(b + 1, last_read["xio"])
                        later("xnorm", norm_x(b + 1))
                    if h == NQ - 2:
                        later("kv", turn_x(0), turn_x(1))
                    if h == NQ - 1:
                        later("kv", make_k(0))
            for ph in range(TT):
                i = TT - 1 - ph
                turned = turns[-1] if turns else None
                leaving = output if ph == 3 else None
                if (n, ph) == (2, 3):
                    at_once(rest)
                    for q in (pe, actq, dve, pool):
                        q.wait(split[-1])
                elif n < 3:
                    next(rest, None)
                    next(rest, None)
                for step in ORDER[ph]:
                    if step == "output_high" and leaving is not None:
                        output_high(leaving)
                    if step == "output_low" and leaving is not None:
                        output_low(leaving)
                    if step == "turned_high" and turned:
                        turned_high(*turned)
                    if step == "turned_low" and turned:
                        turned_low(*turned)
                    if step == "scores" and live:
                        scores(n, i)
                    if step == "exponentials" and live:
                        exponentials(n, i)
                    if step == "normalised":
                        normalised(n, ph)
                    if step == "readers":
                        if ph == 0 and q_parts:
                            at_once(q_parts)
                            q_parts = None
                        elif holding[0]:
                            part(behind, "C")
                if ph == 0 and output is not None:
                    project_out(output)
                    if output % NQ == NQ - 1:
                        assert "tokens" not in tasks, "the batch before's tokens are not through"
                        if output < N - 1:
                            later("tokens", token_layer(output // NQ))
                    output = None
                turns.append((n - 1, i) if 0 < n <= N else None)
                if turns[-1]:
                    turn(n - 1, i)
                for lag in ((5, 4), (4,), (4,), ())[ph]:
                    if len(turns) >= lag and turns[-lag]:
                        values(*turns[-lag])
                        if turns[-lag][1] == 0:
                            output = turns[-lag][0]
                if ph == 3 and n + 2 < N:
                    q_parts = make_q(n + 2)
                    next(q_parts)
                    next(q_parts)
                    part(behind, "C")
                else:
                    part(behind, "PC" if ph or h >= SPARE else "C")
                if ph == 2 and pick_of:
                    m = min(pick_of)
                    if next(pick_of[m], None) is None:
                        del pick_of[m]
        while tasks:
            if not part(["kv", "xnorm", "tokens"], "PC"):
                break
        for m in list(pick_of):
            at_once(pick_of.pop(m))
        heads_through = [(q.sem, q.count) for q in (pe, dve, actq, pool)]
        for q in (pe, dve, actq, pool):
            q.wait(heads_through)

        NP = NE // 2
        s_w = [Slot(sem(f"dma_w{s}")) for s in range(NW)]
        w_read = [None] * NW
        w_in = {}

        def load_expert(e):
            s = e % NW
            if e < NW:
                sp.wait(last_read["xn"] if w_where[s] <= wkv_end else last_read["o"])
            sp.wait(w_read[s])
            for k, w in enumerate((w_gate, w_up)):
                s_w[s].start(sp, w_gu[s][:, :, k * F:(k + 1) * F], w[e].rearrange("(p c) f -> p c f", c=2))
            w_in[e] = s_w[s].start(sp, w_dn[s][0:F2, :, :], w_down[e].rearrange("(p c) h -> p c h", c=2))

        last = NB - 1
        norms = token_norms(last, ("s0", "t0"))
        next(norms)
        next(norms)
        for e in range(NW):
            load_expert(e)
        s_x2in = Slot(sem("dma_x2_in"))
        sp.wait(heads_through, stored["x2"])
        for b in range(last):
            s_x2in.start(sp, fx[b][:], x2_rows[b])
        at_once(norms)
        for _ in zip(route(last, 0, "s0", 0), route(last, 1, "t0", 1), strict=True):
            pass
        picks = pick_of.pop(last)
        for step, _ in enumerate(zip(shared_expert(last, 0, "s1", 0), shared_expert(last, 1, "t1", 1), strict=True)):
            if step % 2:
                next(picks, None)
                next(picks, None)
        at_once(picks)
        stored_rows = [stored["rows"], zt]
        stored_ffn = [stored["ffn", last, 0], stored["ffn", last, 1], zt]

        key = keys[0:NE, 0:CAP]
        dve.wait((dve.sem, dve.count))
        for u in range(2):
            t = dve.done(lambda e, u=u: e.tensor_scalar(tok2[0:NE, u * CAP:(u + 1) * CAP], key, -1.0, float(NT),
                                                        ALU.mult, ALU.add))
        t = dve.done(lambda e: e.scalar_tensor_tensor(out=empty[0:NE, :], in0=key, scalar=0.0,
                                                      in1=slot_row[0:NE, :], op0=ALU.is_equal, op1=ALU.mult))
        dve.wait(t)
        for u in range(2):
            t = dve.done(lambda e, u=u: e.scalar_tensor_tensor(
                out=sct2[0:NE, u * CAP:(u + 1) * CAP], in0=tok2[0:NE, 0:CAP], scalar=float(u * SUMROWS),
                in1=empty[0:NE, :], op0=ALU.add, op1=ALU.add))
        pe.wait(t, free["f"])
        tr(bank["f"][:, 0:NE], tok2[0:NE, :], ident[0:NE, 0:NE])
        t = tr(bank["f"][:, NE:2 * NE], sct2[0:NE, :], ident[0:NE, 0:NE], last=True)
        dve.wait(t)
        for k, o_ in enumerate((idx_g, idx_s)):
            src = bank["f"][:, k * NE:(k + 1) * NE].rearrange("p (j two) -> p j two", two=2)
            for u in range(2):
                rows_ = slice(u * CAP, (u + 1) * CAP)
                t = dve.done(lambda e, o_=o_[rows_, :], i_=src[rows_, :, u]: e.tensor_copy(o_, i_))
        free["f"] = t
        pool.wait(t, stored_rows)

        def vstep(make):
            dve.wait(dve.done(make))

        s_g = [Slot(sem(f"dma_g{i}")) for i in range(NX)]
        s_s = Slot(sem("dma_s"))
        gathered, scattered = {}, {}
        xg_read, made = {}, {}

        def gather(j):
            s = s_g[j % NX]
            pool.wait(xg_read.get(j - NX))
            s.count += 16
            pool.run(lambda e: e.indirect_dma_start(
                xg[j % NX][:], None, table, bass.IndirectOffsetOnAxis(idx_g[:, j:j + 1].bitcast(U32), 0)
            ).then_inc(s.sem, 16))
            gathered[j] = (s.sem, s.count)

        def scatter(j):
            pool.wait(made["d", j], stored_ffn, scattered.get(j - 1))
            s_s.count += 16
            pool.run(lambda e: e.indirect_dma_start(
                sums, bass.IndirectOffsetOnAxis(idx_s[:, j:j + 1].bitcast(U32), 0), dsum[j % ND][:], None,
                compute_op=ALU.add).then_inc(s_s.sem, 16))
            scattered[j] = (s_s.sem, s_s.count)

        def expert_turn(j):
            r, bx = j % 2, f"y{j % 2}"
            pe.wait(gathered[j], free[bx])
            src = xg[j % NX][:, 0:E].rearrange("p (m c) -> p m c", c=EC)
            for c in range(EC):
                t = tr(bank[bx][:, c * P:(c + 1) * P], src[:, :, c], ident[:], last=c == EC - 1)
            actq.wait(t, made.get(("gu", j - 2)))
            t = actq.done(lambda e: e.activation(xt[r][:, :, :].rearrange("p c n -> p (c n)"),
                                                 bank[bx][:, 0:EC * P], ACT.Copy))
            free[bx] = made["xt", j] = t

        def expert_in(j):
            r, bg = j % 2, f"s{j % 2}"
            pe.wait(made["xt", j], free[bg])
            for u in range(2):
                e_ = 2 * j + u
                pe.wait(w_in[e_])
                for c in range(EC):
                    t = mm(bank[bg][u * CAP:(u + 1) * CAP, 0:2 * F], xt[r][:, c, u * CAP:(u + 1) * CAP],
                           w_gu[e_ % NW][:, c, :], start=c == 0, stop=c == EC - 1, last=c == EC - 1)
            made["gu", j] = t

        def expert_act(j):
            r, bg = j % 2, f"s{j % 2}"
            gate, up = bank[bg][:, 0:F], bank[bg][:, F:2 * F]
            x_, a_ = ex[r][:], ag[r][:]
            actq.wait(made["gu", j], made.get(("act", j - 2)))
            t = actq.done(lambda e: e.activation(x_, gate, ACT.Tanh, scale=0.5))
            dve.wait(gathered[j], made.get(("act", j - 2)))
            for u in range(2):
                q = slice(u * CAP, (u + 1) * CAP)
                t2 = dve.done(lambda e, q=q, u=u: e.tensor_scalar(
                    half_w[r][q, :], xg[j % NX][q, E + 2 * j + u:E + 2 * j + u + 1], 0.5, None, ALU.mult))
            xg_read[j] = t2
            dve.wait(t, t2)
            vstep(lambda e: e.scalar_tensor_tensor(out=x_, in0=x_, scalar=1.0, in1=gate, op0=ALU.add, op1=ALU.mult))
            dve.wait(made.get(("at", j - 2)))
            t = dve.done(lambda e: e.scalar_tensor_tensor(out=a_, in0=x_, scalar=half_w[r][:], in1=up,
                                                          op0=ALU.mult, op1=ALU.mult))
            free[bg] = made["act", j] = t

        def activations_turn(j):
            r, ba = j % 2, "of"[j % 2]
            pe.wait(made["act", j], free[ba])
            src = ag[r][:].rearrange("p (m c) -> p m c", c=2)
            for c in range(2):
                t = tr(bank[ba][0:F2, c * P:(c + 1) * P], src[:, :, c], ident[:], last=c == 1)
            made["at", j] = t
            actq.wait(t, made.get(("down", j - 2)))
            t = actq.done(lambda e: e.activation(atr[r][0:F2, :, :].rearrange("p c n -> p (c n)"),
                                                 bank[ba][0:F2, 0:2 * P], ACT.Copy))
            free[ba] = made["atr", j] = t

        def expert_out(j):
            r, bd = j % 2, f"t{j % 2}"
            pe.wait(made["atr", j], free[bd])
            for u in range(2):
                e_ = 2 * j + u
                for c in range(2):
                    t = mm(bank[bd][u * CAP:(u + 1) * CAP, 0:E], atr[r][0:F2, c, u * CAP:(u + 1) * CAP],
                           w_dn[e_ % NW][0:F2, c, :], start=c == 0, stop=c == 1, last=c == 1)
                w_read[e_ % NW] = t
            made["down", j] = t
            actq.wait(t, scattered.get(j - ND))
            t = actq.done(lambda e: e.activation(dsum[j % ND][:], bank[bd][:, 0:E], ACT.Copy))
            free[bd] = made["d", j] = t
            for u in range(2):
                if 2 * j + u + NW < NE:
                    load_expert(2 * j + u + NW)

        for j in range(NX - 1):
            gather(j)
        expert_turn(0)
        expert_turn(1)
        expert_in(0)
        expert_act(0)
        for j in range(NP):
            if j + 2 < NP:
                expert_turn(j + 2)
            activations_turn(j)
            if j + 1 < NP:
                expert_in(j + 1)
                expert_act(j + 1)
            expert_out(j)
            if j + NX - 1 < NP:
                gather(j + NX - 1)
            scatter(j)
            if j == 1:
                sp.wait(stored["x2"])
                x2_in = s_x2in.start(sp, fx[last][:], x2_rows[last])

        s_f = [Slot(sem(f"dma_f{i}")) for i in range(NB)]
        s_o = Slot(sem("dma_out"))
        out_rows = out.rearrange("b (i p) e -> b p i e", p=P)
        sp.wait(scattered[NP - 1])
        arrived, summed, added = {}, {}, {}

        def load_sums(b):
            sp.wait(summed.get(b - NFB))
            s_f[b].start(sp, fa[b][:], sum_rows[0][b])
            arrived[b] = s_f[b].start(sp, fb[b % NFB][:], sum_rows[1][b])

        def add_sums(b):
            pool.wait(arrived[b])
            dve.wait(arrived[b])
            summed[b] = [q.done(lambda e, k=k: e.tensor_tensor(fa[b][:, k, :], fa[b][:, k, :],
                                                               fb[b % NFB][:, k, :], ALU.add))
                         for q, k in ((pool, slice(0, TT - 1)), (dve, slice(TT - 1, TT)))]

        def pair_statistics(p):
            dve.wait(summed[2 * p + 1])
            mean = fmv[p % 2][:, :, 0:1].rearrange("p i o -> p (i o)")
            inv_, bias = fnw[p % 2][:, 1, :], fnw[p % 2][:, 3, :]
            dve.wait(added.get(("norm", 2 * p - 3)))
            pool.wait(added.get(("norm", 2 * p - 3)))
            pool.wait(statistics_now([fa[b][:, k, :] for b in (2 * p, 2 * p + 1) for k in range(TT)],
                                 fstat[p % 2], fmv[p % 2], fnw[p % 2], 0))
            pool.wait(pool.done(lambda e: e.tensor_tensor(bias, mean, inv_, ALU.mult)))
            added["bias", p] = pool.done(lambda e: e.tensor_scalar(bias, bias, -1.0, None, ALU.mult))

        def normalise_out(b):
            nw_, k0 = fnw[b // 2 % 2], b % 2 * TT
            actq.wait(added["bias", b // 2])
            for k in range(TT):
                t = actq.done(lambda e, k=k: e.activation(fa[b][:, k, :], fa[b][:, k, :], ACT.Identity,
                                                          scale=nw_[:, 1, k0 + k:k0 + k + 1],
                                                          bias=nw_[:, 3, k0 + k:k0 + k + 1]))
            added["norm", b] = t

        def residual_out(b):
            dve.wait(added["norm", b], x2_in)
            t = dve.done(lambda e: e.tensor_tensor(fa[b][:], fa[b][:], fx[b][:], ALU.add))
            sp.wait(t)
            added["out"] = s_o.start(sp, out_rows[b], fa[b][:])

        for b in range(min(NFB, NB)):
            load_sums(b)
        add_sums(0)
        add_sums(1)
        for p in range(NB // 2):
            for b in (2 * p + 2, 2 * p + 3):
                if b < NB:
                    add_sums(b)
                if b - 2 + NFB < NB:
                    load_sums(b - 2 + NFB)
            pair_statistics(p)
            normalise_out(2 * p)
            normalise_out(2 * p + 1)
            if p:
                residual_out(2 * p - 2)
                residual_out(2 * p - 1)
        residual_out(NB - 2)
        residual_out(NB - 1)
        sp.wait(added["out"])

        block = ctx.enter_context(nc.Block())

        @block.sync
        def _(e):
            sp.emit(e)

        @block.gpsimd
        def _(e):
            pool.emit(e)

        @block.scalar
        def _(e):
            actq.emit(e)

        @block.vector
        def _(e):
            dve.emit(e)

        @block.tensor
        def _(e):
            pe.emit(e)


def shape_constants(T, d, NT, cap):
    import numpy as np
    half = T // 2
    pos = np.arange(T, dtype=np.float32)[:, None]
    i = np.arange(0, d, 2, dtype=np.float32)
    inv_freq = np.exp(-(np.log(np.float32(10000.0)) * i / np.float32(d))).astype(np.float32)
    ang = (pos * inv_freq).astype(np.float32)
    pe = np.zeros((T, d), np.float32)
    pe[:, 0::2], pe[:, 1::2] = np.sin(ang), np.cos(ang)
    ident = np.eye(d, dtype=np.float32)
    pe_t = (pe.T * np.float32(float(d) ** -0.25)).astype(np.float32)
    keys = np.broadcast_to(-np.arange(half, dtype=np.float32), (d, half))
    slots = np.broadcast_to(np.arange(cap, dtype=np.float32), (d, cap))
    causal = np.where(np.arange(d)[None, :] > np.arange(d)[:, None], MASKED, 0.0).astype(np.float32)
    return np.ascontiguousarray(np.concatenate([ident, pe_t, keys, slots, causal], axis=1))


def kernel(**inputs):
    import numpy as np
    import concourse.bacc as bacc
    from concourse.bass_utils import run_bass_kernel_spmd

    a = {k: np.asarray(v) for k, v in inputs.items()}
    x = a["L0_attn_x"]
    B, T, E = x.shape
    nq = a["L0_attn_wq"].shape[1] // P
    arrays = {
        "x": x,
        "wq": a["L0_attn_wq"],
        "bqT": a["L0_attn_bq"].reshape(nq, P).T,
        "wkv": a["L0_attn_wkv"],
        "bkvT": a["L0_attn_bkv"].reshape(-1, P).T,
        "wo": a["L0_attn_wo"],
        "gwT": a["L0_ffn_gate_w"].T,
        "w_gate": a["L0_ffn_w_gate"],
        "w_up": a["L0_ffn_w_up"],
        "w_down": a["L0_ffn_w_down"],
        "sgT": a["L0_ffn_sh_gate"].T,
        "suT": a["L0_ffn_sh_up"].T,
        "sdT": a["L0_ffn_sh_down"].T,
        "consts": shape_constants(T, P, B * T, CAP),
    }
    arrays = {k: np.ascontiguousarray(v) for k, v in arrays.items()}
    nc = bacc.Bacc("TRN2", target_bir_lowering=False, num_devices=1)
    args = [nc.dram_tensor(f"in_{k}", v.shape, mybir.dt.from_np(v.dtype), kind="ExternalInput").ap()
            for k, v in arrays.items()]
    out = nc.dram_tensor("out_0", x.shape, F32, kind="ExternalOutput").ap()
    build(nc, *args, out)
    r = run_bass_kernel_spmd(nc, [{f"in_{k}": v for k, v in arrays.items()}], core_ids=[0])
    return r.results[0]["out_0"]
```
